# Optimizing a Trainium2 kernel written in Bass

```python
import numpy as np
import jax
import jax.numpy as jnp

def _softmax(x, axis=-1):
    return jax.nn.softmax(x, axis=axis)

def _gelu(x):
    return jax.nn.gelu(x, approximate=True)

def _silu(x):
    return jax.nn.silu(x)

def _sigmoid(x):
    return jax.nn.sigmoid(x)

def _layernorm(x, axis=-1, eps=1e-05):
    m = jnp.mean(x, axis=axis, keepdims=True)
    v = jnp.var(x, axis=axis, keepdims=True)
    return (x - m) / jnp.sqrt(v + eps)

def _scatter_add(tgt, idx, src, axis=0):
    return tgt.at[idx].add(src)

def _segment_sum(src, seg, n):
    return jax.ops.segment_sum(src, seg, n)
kernel_name = 'mk_gnn_resnorm_d1_gnn_r8_823984'

def setup_inputs(seed: int=0):
    np.random.seed(seed)
    _w = jnp.asarray

    def _rec_inputs():
        import jax
        import jax.numpy as jnp
        _gk = jax.random.key(seed)
        x = -0.000202 + 1 * jax.random.normal(jax.random.fold_in(_gk, 1), (6250, 128), jnp.float32)
        src = jax.random.randint(jax.random.fold_in(_gk, 2), (100000,), 0, 6250, jnp.int32)
        dst = jax.random.randint(jax.random.fold_in(_gk, 3), (100000,), 0, 6250, jnp.int32)
        _o = jnp.argsort(dst, stable=True)
        src = src[_o]
        dst = dst[_o]
        edge_attr_128 = -8.16379e-05 + 0.999858 * jax.random.normal(jax.random.fold_in(_gk, 12), (100000, 128), jnp.float32)
        return (x, src, dst, edge_attr_128)
    x, src, dst, edge_attr_128 = _rec_inputs()

    def _L0_gnn_setup():
        import jax, jax.numpy as jnp
        import numpy as np
        N_NODES = 6250
        N_EDGES = 100000
        D = 128
        RRELU_SLOPE = (1.0 / 8.0 + 1.0 / 3.0) / 2.0

        def _layer(h, edge_feats, src, dst, deg, iso, Wn, Ws, Wi, num_nodes):
            msg = (h[src] + edge_feats) @ Wn.T
            agg = jax.ops.segment_sum(msg, dst, num_segments=num_nodes)
            agg = agg / jnp.maximum(deg, 1.0)[:, None]
            self_msg = jnp.where(iso[:, None], h @ Wi.T, h @ Ws.T)
            x = agg + self_msg
            return jnp.where(x >= 0, x, RRELU_SLOPE * x)
        key = jax.random.key(seed)
        ks = jax.random.split(key, 10)
        s = 1.0 / np.sqrt(D)
        return {'node_feats': jax.random.normal(ks[0], (N_NODES, D), dtype=jnp.float32), 'edge_feats': jax.random.normal(ks[1], (N_EDGES, D), dtype=jnp.float32), 'src': jax.random.randint(ks[2], (N_EDGES,), 0, N_NODES, dtype=jnp.int32), 'dst': jax.random.randint(ks[3], (N_EDGES,), 0, N_NODES, dtype=jnp.int32), 'Wn0': jax.random.uniform(ks[4], (D, D), jnp.float32, -s, s), 'Ws0': jax.random.uniform(ks[5], (D, D), jnp.float32, -s, s), 'Wi0': jax.random.uniform(ks[6], (D, D), jnp.float32, -s, s), 'Wn1': jax.random.uniform(ks[7], (D, D), jnp.float32, -s, s), 'Ws1': jax.random.uniform(ks[8], (D, D), jnp.float32, -s, s), 'Wi1': jax.random.uniform(ks[9], (D, D), jnp.float32, -s, s)}
    _L0_gnn_all = _L0_gnn_setup()
    _L0_gnn_in = {k: v for k, v in _L0_gnn_all.items() if k in ('Wn0', 'Ws0', 'Wi0', 'Wn1', 'Ws1', 'Wi1')}
    del _L0_gnn_all
    return {'x': x, 'src': src, 'dst': dst, 'edge_attr_128': edge_attr_128, 'L0_gnn_Wn0': _L0_gnn_in['Wn0'], 'L0_gnn_Ws0': _L0_gnn_in['Ws0'], 'L0_gnn_Wi0': _L0_gnn_in['Wi0'], 'L0_gnn_Wn1': _L0_gnn_in['Wn1'], 'L0_gnn_Ws1': _L0_gnn_in['Ws1'], 'L0_gnn_Wi1': _L0_gnn_in['Wi1']}

def reference(x, src, dst, edge_attr_128, L0_gnn_Wn0, L0_gnn_Ws0, L0_gnn_Wi0, L0_gnn_Wn1, L0_gnn_Ws1, L0_gnn_Wi1):
    import jax
    import jax.numpy as jnp

    def _L0_gnn_ref(node_feats, edge_feats, src, dst, Wn0, Ws0, Wi0, Wn1, Ws1, Wi1):
        import jax, jax.numpy as jnp
        import numpy as np
        N_NODES = 6250
        N_EDGES = 100000
        D = 128
        RRELU_SLOPE = (1.0 / 8.0 + 1.0 / 3.0) / 2.0

        def _layer(h, edge_feats, src, dst, deg, iso, Wn, Ws, Wi, num_nodes):
            msg = (h[src] + edge_feats) @ Wn.T
            agg = jax.ops.segment_sum(msg, dst, num_segments=num_nodes)
            agg = agg / jnp.maximum(deg, 1.0)[:, None]
            self_msg = jnp.where(iso[:, None], h @ Wi.T, h @ Ws.T)
            x = agg + self_msg
            return jnp.where(x >= 0, x, RRELU_SLOPE * x)
        num_nodes = node_feats.shape[0]
        deg = jax.ops.segment_sum(jnp.ones(src.shape[0], dtype=node_feats.dtype), dst, num_segments=num_nodes)
        iso = deg == 0
        h = _layer(node_feats, edge_feats, src, dst, deg, iso, Wn0, Ws0, Wi0, num_nodes)
        h = _layer(h, edge_feats, src, dst, deg, iso, Wn1, Ws1, Wi1, num_nodes)
        return h
    x = _layernorm(x + _L0_gnn_ref(x, edge_attr_128, src, dst, L0_gnn_Wn0, L0_gnn_Ws0, L0_gnn_Wi0, L0_gnn_Wn1, L0_gnn_Ws1, L0_gnn_Wi1), axis=-1)
    return x

_drawn_inputs = setup_inputs


def setup_inputs(seed=0):
    import zlib

    import numpy as np

    out = dict(_drawn_inputs(seed))
    spreads = {}
    factors = {}
    for name, (base, spread) in spreads.items():
        noise = np.random.default_rng([zlib.crc32(name.encode()), seed]).standard_normal(out[name].shape)
        drawn = base * np.exp(spread * noise) if base else spread * noise
        out[name] = jnp.asarray(drawn.astype(out[name].dtype))
    for name, factor in factors.items():
        out[name] = (out[name] * factor).astype(out[name].dtype)
    return out
```

```python
import concourse.bass as bass
from concourse import mybir
from contextlib import ExitStack


def gnn_resnorm_kernel(nc, x_rows, x_cols, src, dst, edges, wn0, ws0, wi0, wn1, ws1, wi1, out):
    f32, i32 = mybir.dt.float32, mybir.dt.int32
    ALU, ACT, AX = mybir.AluOpType, mybir.ActivationFunctionType, mybir.AxisListType
    EPS = 1e-5
    SLOPE = (1.0 / 8.0 + 1.0 / 3.0) / 2.0

    P = 128
    D = x_rows.shape[1]
    N = out.shape[0]
    TILES = x_rows.shape[0] // P
    NP = TILES * P
    CHUNKS = src.shape[1]
    SUB = 4
    SLOTS = 4
    GC = SUB * SLOTS
    GROUPS = CHUNKS // GC
    W = 64
    WINDOWS = NP // W
    TAIL = N - (TILES - 1) * P
    assert GROUPS == TILES and CHUNKS % GC == 0

    h1_rows = nc.dram_tensor("h1_rows", (NP, D), f32, kind="Internal").ap()

    ctx = ExitStack()
    with ctx:
        def sb(name, shape, dt=f32):
            return ctx.enter_context(nc.sbuf_tensor(name, shape, dt))

        def sem(name):
            return ctx.enter_context(nc.semaphore(name))

        src_idx = sb("src_idx", [P, CHUNKS + GC], i32)
        dst_idx = sb("dst_idx", [P, CHUNKS + GC], i32)
        dst_f = sb("dst_f", [P, CHUNKS + GC])
        rel = sb("rel", [P, CHUNKS + GC])
        first_dst = sb("first_dst", [P, CHUNKS])
        bad_a = sb("bad_a", [P, CHUNKS])
        bad_b = sb("bad_b", [P, CHUNKS])
        bad_sum = sb("bad_sum", [P, 1])
        base_f = sb("base_f", [1, GROUPS * SLOTS])
        base_i = sb("base_i", [1, GROUPS * SLOTS], i32)
        general = sb("general", [1, 1], i32)
        ones = sb("ones", [P, P])
        zeros = sb("zeros", [P, P])
        column = sb("column", [P, W])
        lane = sb("lane", [P, P])
        ident = sb("ident", [P, P])

        EDGE, ROW, DEG = range(3)
        sums = sb("sums", [P, 3, NP])
        h_cols = sb("h_cols", [P, NP])

        idx = sb("idx", [P, GC], i32)
        rows = sb("rows", [P, GC, D])
        feats = sb("feats", [P, GC, D])
        onehot = sb("onehot", [P, GC, W])
        rel_w = sb("rel_w", [P, GC])

        wts = sb("wts", [P, 6, D])
        agg = sb("agg", [P, P])
        agg_mean = sb("agg_mean", [P, P])
        deg_1 = sb("deg_1", [P, P])
        deg_r = sb("deg_r", [P, P])
        iso = sb("iso", [P, P])
        h_iso = sb("h_iso", [P, P])
        h_con = sb("h_con", [P, P])
        leaked = sb("leaked", [P, D])
        h_row = sb("h_row", [P, D])
        x_tile = sb("x_tile", [P, D])
        res = sb("res", [P, D])
        stats = sb("stats", [P, 6])
        mv = sb("mv", [P, 2])
        std = sb("std", [P, 1])
        rstd = sb("rstd", [P, 1])
        eps = sb("eps", [P, 1])
        y_row = sb("y_row", [P, D])

        ps_win = [ctx.enter_context(nc.psum_tensor(f"ps_win{i}", [P, 512], f32)) for i in range(2)]
        ps_node = ctx.enter_context(nc.psum_tensor("ps_node", [P, 512], f32))
        ps_t = ctx.enter_context(nc.psum_tensor("ps_t", [P, 512], f32))
        ps_set = ctx.enter_context(nc.psum_tensor("ps_set", [P, 512], f32))

        in_loaded = sem("in_loaded")
        tables_made = sem("tables_made")
        setup_step = sem("setup_step")
        bases_spread = sem("bases_spread")
        bad_counted = sem("bad_counted")
        setup_done = sem("setup_done")
        idx_ready = sem("idx_ready")
        onehot_ready = sem("onehot_ready")
        rows_gathered = [sem(f"rows_gathered{j}") for j in range(SLOTS)]
        feats_loaded = [sem(f"feats_loaded{j}") for j in range(SLOTS)]
        window_summed = sem("window_summed")
        window_added = sem("window_added")
        pool_step = sem("pool_step")
        pe_step = sem("pe_step")
        dve_step = sem("dve_step")
        rel_ready = sem("rel_ready")
        agg_summed = sem("agg_summed")
        sums_cleared = sem("sums_cleared")
        deg_clamped = sem("deg_clamped")
        deg_inverted = sem("deg_inverted")
        iso_split = sem("iso_split")
        node_in = sem("node_in")
        node_out = sem("node_out")
        leak_made = sem("leak_made")
        h_made = sem("h_made")
        h_turned = sem("h_turned")
        h_kept = sem("h_kept")
        h_stored = sem("h_stored")
        x_loaded = sem("x_loaded")
        res_made = sem("res_made")
        stats_made = sem("stats_made")
        mv_made = sem("mv_made")
        std_made = sem("std_made")
        rstd_made = sem("rstd_made")
        y_made = sem("y_made")
        out_stored = sem("out_stored")

        block = ctx.enter_context(nc.Block())

        def at(v, n=1):
            return bass.ds(v, n)

        def load_flag(engine):
            return nc.values_load(general[0:1, 0:1], engines=(engine,), min_val=0, max_val=1)

        N_IN = 10

        @block.sync
        def _(sp):
            sp.dma_start(dst_idx[:, 0:CHUNKS], dst[:, :]).then_inc(in_loaded, 16)
            sp.dma_start(dst_idx[:, CHUNKS:], dst[:, 0:GC]).then_inc(in_loaded, 16)
            sp.dma_start(src_idx[:, 0:CHUNKS], src[:, :]).then_inc(in_loaded, 16)
            sp.dma_start(src_idx[:, CHUNKS:], src[:, 0:GC]).then_inc(in_loaded, 16)
            for k, w in enumerate((wn0, ws0, wi0, wn1, ws1, wi1)):
                sp.dma_start(wts[:, k, :], w[:, :]).then_inc(in_loaded, 16)
            sp.dma_start(h_cols[:, :], x_cols[:, :]).then_inc(in_loaded, 16)

            def load_feats(g, j):
                sp.dma_start(feats[:, SUB * j:SUB * (j + 1), :],
                             edges[:, at(g * GC + SUB * j, SUB), :]).then_inc(feats_loaded[j], 16)

            def load_x(t):
                if not isinstance(t, int) or t > 0:
                    sp.wait_ge(res_made, t)
                sp.dma_start(x_tile[:, :], x_rows[at(t * P, P), :]).then_inc(x_loaded, 16)

            sp.wait_ge(setup_done, 1)
            flag = load_flag(mybir.EngineType.SP)
            with sp.If(flag == 0):
                for j in range(SLOTS):
                    load_feats(0, j)
                with sp.Fori(1, GROUPS) as g:
                    for j in range(SLOTS):
                        sp.wait_ge(window_summed, (g - 1) * SLOTS + j + 1)
                        load_feats(g, j)
            with sp.Else():
                for j in range(SLOTS):
                    load_feats(0, j)
                with sp.Fori(1, GROUPS) as g:
                    sp.wait_ge(window_summed, g * WINDOWS + 1)
                    for j in range(SLOTS):
                        load_feats(g, j)
            load_x(0)
            with sp.Fori(1, TILES) as t:
                load_x(t)

        @block.gpsimd
        def _(pool):
            nc.gpsimd.iota(column[:, :], [[1, W]], base=0, channel_multiplier=0,
                           allow_small_or_imprecise_dtypes=True).then_inc(tables_made, 1)
            nc.gpsimd.iota(first_dst[:, :], [[P, GROUPS], [0, GC]], base=-P, channel_multiplier=0,
                           allow_small_or_imprecise_dtypes=True).then_inc(tables_made, 1)
            nc.gpsimd.iota(lane[:, :], [[1, P]], base=0, channel_multiplier=-1,
                           allow_small_or_imprecise_dtypes=True).then_inc(tables_made, 1)

            def gather(table, layer_groups, g, j):
                pool.wait_ge(idx_ready, (layer_groups + g) * SLOTS + j + 1)
                pool.sem_inc(pool_step, 1)
                for c in range(SUB * j, SUB * (j + 1)):
                    nc.gpsimd.indirect_dma_start(
                        rows[:, c, :], None, table[:, :],
                        bass.IndirectOffsetOnAxis(ap=idx[:, c:c + 1], axis=0)).then_inc(rows_gathered[j], 16)

            for layer, table in enumerate((x_rows, h1_rows)):
                if layer:
                    pool.wait_ge(h_stored, 16 * TILES)
                    pool.sem_inc(pool_step, 1)
                with pool.Fori(0, GROUPS) as g:
                    for j in range(SLOTS):
                        gather(table, layer * GROUPS, g, j)

        @block.vector
        def _(dve):
            nc.vector.memset(ones[:, :], 1.0)
            nc.vector.memset(eps[:, :], EPS)
            nc.vector.memset(zeros[:, :], 0.0)
            nc.vector.memset(sums[:, :, :], 0.0).then_inc(setup_step, 1)
            dve.wait_ge(in_loaded, 16 * (N_IN + 1))
            nc.vector.tensor_copy(dst_f[:, :], dst_idx[:, :]).then_inc(setup_step, 1)
            dve.wait_ge(tables_made, 3)
            nc.vector.tensor_single_scalar(ident[:, :], lane[:, :], 0.0, ALU.is_equal).then_inc(setup_step, 1)
            dve.wait_ge(setup_step, 2)
            nc.vector.tensor_scalar(base_f[0:1, :],
                                    dst_f[0:1, 0:CHUNKS].rearrange("p (s c) -> p s c", c=SUB)[:, :, 0],
                                    float(NP - W), None, ALU.min).then_inc(setup_step, 1)
            dve.wait_ge(setup_step, 4)
            nc.vector.tensor_copy(base_i[0:1, :], base_f[0:1, :]).then_inc(setup_step, 1)
            dve.wait_ge(bases_spread, 1)
            NB = GROUPS * SLOTS
            nc.vector.tensor_tensor(rel[:, 0:CHUNKS].rearrange("p (s c) -> p s c", c=SUB),
                                    dst_f[:, 0:CHUNKS].rearrange("p (s c) -> p s c", c=SUB),
                                    ps_set[:, 0:NB].unsqueeze(2).to_broadcast([P, NB, SUB]),
                                    ALU.subtract).then_inc(setup_step, 1)
            nc.vector.tensor_single_scalar(bad_a[:, :], dst_f[:, 0:CHUNKS], float(N), ALU.is_lt).then_inc(setup_step, 1)
            dve.wait_ge(setup_step, 7)
            nc.vector.tensor_copy(rel[:, CHUNKS:], rel[:, 0:GC]).then_inc(setup_step, 1)
            nc.vector.scalar_tensor_tensor(bad_b[:, :], rel[:, 0:CHUNKS], float(W), bad_a[:, :],
                                           ALU.is_ge, ALU.mult).then_inc(setup_step, 1)
            dve.wait_ge(setup_step, 9)
            nc.vector.scalar_tensor_tensor(bad_a[:, :], rel[:, 0:CHUNKS], 0.0, bad_b[:, :],
                                           ALU.is_lt, ALU.add).then_inc(setup_step, 1)
            dve.wait_ge(setup_step, 10)
            nc.vector.tensor_tensor(bad_b[:, :], dst_f[:, 0:CHUNKS], first_dst[:, :], ALU.is_lt).then_inc(setup_step, 1)
            dve.wait_ge(setup_step, 11)
            nc.vector.tensor_tensor(first_dst[:, :], bad_a[:, :], bad_b[:, :], ALU.max).then_inc(setup_step, 1)
            dve.wait_ge(setup_step, 12)
            nc.vector.reduce_max(bad_sum[:, :], first_dst[:, :], AX.X).then_inc(setup_step, 1)
            dve.wait_ge(bad_counted, 1)
            nc.vector.tensor_scalar(general[0:1, 0:1], ps_set[0:1, 256:257], 1.0, None, ALU.min).then_inc(setup_done, 1)

            def prepare(groups_before, g, j):
                nc.vector.tensor_copy(idx[:, SUB * j:SUB * (j + 1)],
                                      src_idx[:, at(g * GC + SUB * j, SUB)]).then_inc(idx_ready, 1)
                for c in range(SUB):
                    k = SUB * j + c
                    last = nc.vector.tensor_scalar(onehot[:, k, :], column[:, :], rel[:, at(g * GC + k)],
                                                   None, ALU.is_equal)
                last.then_inc(onehot_ready, 1)

            def add_window(layer, at_node, ps):
                what = (slice(0, 3), 3) if layer == 0 else (slice(ROW, ROW + 1), 1)
                s = sums[:, what[0], at(at_node, W)]
                p = ps[:, what[0].start * W:what[0].stop * W].rearrange("p (k w) -> p k w", w=W)
                return nc.vector.tensor_tensor(s, s, p, ALU.add)

            def node_inputs(layer, t):
                n = layer * TILES + t
                tile = at(t * P, P)
                deg = sums[:, DEG, tile]
                if layer or not isinstance(t, int) or t > 0:
                    dve.wait_ge(node_out, n)
                nc.vector.tensor_tensor(agg[:, :], sums[:, EDGE, tile], sums[:, ROW, tile],
                                        ALU.add).then_inc(agg_summed, 1)
                nc.vector.tensor_scalar_max(deg_1[:, :], deg, 1.0).then_inc(deg_clamped, 1)
                nc.vector.tensor_single_scalar(iso[:, :], deg, 0.0, ALU.is_equal).then_inc(iso_split, 1)
                dve.wait_ge(deg_clamped, n + 1)
                nc.vector.reciprocal(deg_r[:, :], deg_1[:, :]).then_inc(deg_inverted, 1)
                dve.wait_ge(iso_split, 2 * n + 1)
                if layer:
                    dve.wait_ge(h_kept, TILES)
                nc.vector.tensor_tensor(h_iso[:, :], h_cols[:, tile], iso[:, :], ALU.mult).then_inc(iso_split, 1)
                dve.wait_ge(deg_inverted, n + 1)
                nc.vector.tensor_tensor(agg_mean[:, :], agg[:, :], deg_r[:, :], ALU.mult).then_inc(node_in, 1)
                dve.wait_ge(iso_split, 2 * n + 2)
                nc.vector.tensor_tensor(h_con[:, :], h_cols[:, tile], h_iso[:, :], ALU.subtract).then_inc(node_in, 1)
                if layer == 0:
                    dve.wait_ge(agg_summed, n + 1)
                    nc.vector.tensor_tensor(sums[:, ROW, tile], zeros[:, :], zeros[:, :], ALU.add).then_inc(sums_cleared, 1)

            def activate(layer, t):
                n = layer * TILES + t
                if layer == 0 and (not isinstance(t, int) or t > 0):
                    dve.wait_ge(h_stored, 16 * t)
                    dve.wait_ge(h_turned, t)
                elif layer and isinstance(t, int) and t == 0:
                    dve.wait_ge(h_stored, 16 * TILES)
                    dve.wait_ge(h_turned, TILES)
                elif layer:
                    dve.wait_ge(res_made, t)
                dve.wait_ge(leak_made, n + 1)
                nc.vector.tensor_tensor(h_row[:, :], ps_node[:, 0:D], leaked[:, :], ALU.max).then_inc(h_made, 1)

            def finish(t):
                dve.wait_ge(h_made, TILES + t + 1)
                dve.wait_ge(x_loaded, 16 * (t + 1))
                nc.vector.tensor_tensor(res[:, :], h_row[:, :], x_tile[:, :], ALU.add).then_inc(res_made, 1)
                dve.wait_ge(res_made, t + 1)
                nc.vector.bn_stats(stats[:, :], res[:, :]).then_inc(stats_made, 1)
                dve.wait_ge(stats_made, t + 1)
                dve.sem_inc(dve_step, 1)
                nc.vector.bn_aggr(mv[:, :], stats[:, :]).then_inc(mv_made, 1)
                dve.wait_ge(std_made, t + 1)
                nc.vector.reciprocal(rstd[:, :], std[:, :]).then_inc(rstd_made, 1)
                dve.wait_ge(rstd_made, t + 1)
                if not isinstance(t, int) or t > 0:
                    dve.wait_ge(out_stored, 16 * t)
                nc.vector.tensor_scalar(y_row[:, :], res[:, :], mv[:, 0:1], rstd[:, :],
                                        ALU.subtract, ALU.mult).then_inc(y_made, 1)

            def ordered_group(layer, g):
                bases = nc.values_load_multi_w_load_instructions(
                    base_i[0:1, at(g * SLOTS, SLOTS)], (mybir.EngineType.DVE,), min_val=0, max_val=NP - W,
                    skip_runtime_bounds_check_because="the setup keeps the bases within 0 .. NP - W")[1]
                for j in range(SLOTS):
                    n = (layer * GROUPS + g) * SLOTS + j
                    dve.wait_ge(window_summed, n + 1)
                    if layer or not (isinstance(g, int) and g == 0 and j == 0):
                        dve.wait_ge(window_added, n)
                    add_window(layer, bases[j], ps_win[j % 2]).then_inc(window_added, 1)
                    prepare(layer * GROUPS, g + 1, j)

            def tried_group(layer, g):
                before = (layer * GROUPS + g) * WINDOWS
                dve.wait_ge(window_summed, before + 1)
                dve.wait_ge(rel_ready, before + layer * GROUPS + g + 1)
                nc.vector.tensor_copy(idx[:, :], src_idx[:, at(g * GC, GC)]).then_inc(idx_ready, SLOTS)
                nc.vector.tensor_copy(rel_w[:, :], dst_f[:, at(g * GC, GC)]).then_inc(rel_ready, 1)
                with dve.Fori(0, WINDOWS) as w:
                    n = before + w
                    dve.wait_ge(window_summed, n + 1)
                    dve.wait_ge(rel_ready, n + layer * GROUPS + g + 2)
                    for k in range(GC):
                        last = nc.vector.tensor_scalar(onehot[:, k, :], column[:, :], rel_w[:, k:k + 1],
                                                       None, ALU.is_equal)
                    last.then_inc(onehot_ready, 1)
                    dve.wait_ge(onehot_ready, n + 1)
                    nc.vector.tensor_scalar(rel_w[:, :], rel_w[:, :], float(W), None,
                                            ALU.subtract).then_inc(rel_ready, 1)
                    dve.wait_ge(window_summed, n + 2)
                    add_window(layer, w * W, ps_win[0]).then_inc(window_added, 1)

            def node_tile(layer, t):
                node_inputs(layer, t)
                activate(layer, t)
                if layer:
                    finish(t)

            dve.wait_ge(setup_done, 1)
            flag = load_flag(mybir.EngineType.DVE)
            with dve.If(flag == 0):
                for j in range(SLOTS):
                    prepare(0, 0, j)
                for layer in range(2):
                    ordered_group(layer, 0)
                    with dve.Fori(1, GROUPS) as g:
                        ordered_group(layer, g)
                        dve.wait_ge(window_added, (layer * GROUPS + g + 1) * SLOTS)
                        node_tile(layer, g - 1)
                    node_tile(layer, TILES - 1)
            with dve.Else():
                dve.sem_inc(window_summed, 1)
                dve.sem_inc(window_added, 1)
                dve.sem_inc(rel_ready, 1)
                for layer in range(2):
                    with dve.Fori(0, GROUPS) as g:
                        tried_group(layer, g)
                    dve.wait_ge(window_added, (layer + 1) * GROUPS * WINDOWS + 1)
                    node_tile(layer, 0)
                    with dve.Fori(1, TILES) as t:
                        node_tile(layer, t)
                    if layer == 0:
                        dve.wait_ge(sums_cleared, TILES)

        @block.scalar
        def _(act):
            def leak(layer, t):
                n = layer * TILES + t
                act.wait_ge(node_out, n + 1)
                if layer or not isinstance(t, int) or t > 0:
                    act.wait_ge(h_made, n)
                nc.scalar.mul(leaked[:, :], ps_node[:, 0:D], SLOPE).then_inc(leak_made, 1)

            def keep(t):
                act.wait_ge(h_made, t + 1)
                act.dma_start(h1_rows[at(t * P, P), :], h_row[:, :]).then_inc(h_stored, 16)
                act.wait_ge(h_turned, t + 1)
                nc.scalar.copy(h_cols[:, at(t * P, P)], ps_t[:, 0:P]).then_inc(h_kept, 1)

            def root(t):
                act.wait_ge(mv_made, t + 1)
                nc.scalar.activation(std[:, :], mv[:, 1:2], ACT.Sqrt, bias=eps[:, :]).then_inc(std_made, 1)

            def store(t, n):
                act.wait_ge(y_made, t + 1)
                act.dma_start(out[at(t * P, n), :], y_row[0:n, :]).then_inc(out_stored, 16)

            leak(0, 0)
            keep(0)
            with act.Fori(1, TILES) as t:
                leak(0, t)
                keep(t)
            act.wait_ge(h_stored, 16 * TILES)
            leak(1, 0)
            root(0)
            store(0, P)
            with act.Fori(1, TILES - 1) as t:
                leak(1, t)
                root(t)
                store(t, P)
            leak(1, TILES - 1)
            root(TILES - 1)
            store(TILES - 1, TAIL)
            act.wait_ge(out_stored, 16 * TILES)

        @block.tensor
        def _(pe):
            pe.wait_ge(setup_step, 4)
            nc.tensor.matmul(ps_set[:, 0:GROUPS * SLOTS], ones[0:1, :], base_f[0:1, :],
                             start=True, stop=True).then_inc(bases_spread, 1)
            pe.wait_ge(setup_step, 13)
            nc.tensor.matmul(ps_set[0:1, 256:257], bad_sum[:, :], ones[:, 0:1],
                             start=True, stop=True).then_inc(bad_counted, 1)

            def sum_chunks(layer, ps, ks):
                for what, left in ((EDGE, lambda k: feats[:, k, :]), (ROW, lambda k: rows[:, k, :]),
                                   (DEG, lambda k: ones[:, :])):
                    if layer and what != ROW:
                        continue
                    for k in ks:
                        last = nc.tensor.matmul(ps[:, what * W:(what + 1) * W], left(k), onehot[:, k, :],
                                                start=(k == ks[0]), stop=(k == ks[-1]))
                return last

            def ordered_group(layer, g):
                for j in range(SLOTS):
                    n = (layer * GROUPS + g) * SLOTS + j
                    pe.wait_ge(onehot_ready, n + 1)
                    if layer == 0:
                        pe.wait_ge(feats_loaded[j], 16 * (g + 1))
                    pe.wait_ge(rows_gathered[j], 16 * SUB * (layer * GROUPS + g + 1))
                    if layer or not (isinstance(g, int) and g == 0 and j < 2):
                        pe.wait_ge(window_added, n - 1)
                    sum_chunks(layer, ps_win[j % 2], range(SUB * j, SUB * (j + 1))).then_inc(window_summed, 1)

            def tried_group(layer, g):
                for j in range(SLOTS):
                    if layer == 0:
                        pe.wait_ge(feats_loaded[j], 16 * (g + 1))
                    pe.wait_ge(rows_gathered[j], 16 * SUB * (layer * GROUPS + g + 1))
                pe.sem_inc(pe_step, 1)
                with pe.Fori(0, WINDOWS) as w:
                    n = (layer * GROUPS + g) * WINDOWS + w
                    pe.wait_ge(onehot_ready, n + 1)
                    pe.wait_ge(window_added, n + 1)
                    sum_chunks(layer, ps_win[0], range(GC)).then_inc(window_summed, 1)

            def node_tile(layer, t):
                n = layer * TILES + t
                pe.wait_ge(node_in, 2 * (n + 1))
                if layer or not isinstance(t, int) or t > 0:
                    pe.wait_ge(h_made, n)
                for k, left in enumerate((agg_mean, h_con, h_iso)):
                    last = nc.tensor.matmul(ps_node[:, 0:D], left[:, :], wts[:, 3 * layer + k, :],
                                            start=(k == 0), stop=(k == 2))
                last.then_inc(node_out, 1)
                if layer == 0:
                    pe.wait_ge(h_made, t + 1)
                    if not isinstance(t, int) or t > 0:
                        pe.wait_ge(h_kept, t)
                    nc.tensor.transpose(ps_t[:, 0:P], h_row[:, :], ident[:, :]).then_inc(h_turned, 1)

            pe.wait_ge(setup_done, 1)
            flag = load_flag(mybir.EngineType.PE)
            with pe.If(flag == 0):
                for layer in range(2):
                    ordered_group(layer, 0)
                    with pe.Fori(1, GROUPS) as g:
                        ordered_group(layer, g)
                        node_tile(layer, g - 1)
                    node_tile(layer, TILES - 1)
            with pe.Else():
                for layer in range(2):
                    with pe.Fori(0, GROUPS) as g:
                        tried_group(layer, g)
                    node_tile(layer, 0)
                    with pe.Fori(1, TILES) as t:
                        node_tile(layer, t)


_ORDER = ["x_rows", "x_cols", "src", "dst", "edges", "wn0", "ws0", "wi0", "wn1", "ws1", "wi1"]


def kernel(**inputs):
    import numpy as _np
    import concourse.bacc as _bacc
    from concourse import mybir as _mybir
    from concourse.bass_utils import run_bass_kernel_spmd as _run

    x = _np.asarray(inputs["x"])
    src, dst = _np.asarray(inputs["src"]), _np.asarray(inputs["dst"])
    feats = _np.asarray(inputs["edge_attr_128"])
    P, GROUP = 128, 2048
    n, e = x.shape[0], src.shape[0]
    n_pad, e_pad = -n % P, -e % GROUP
    x_rows = _np.pad(x, ((0, n_pad), (0, 0)))
    lay = {
        "x_rows": x_rows,
        "x_cols": x_rows.T,
        "src": _np.pad(src, (0, e_pad)).reshape(-1, P).T,
        "dst": _np.pad(dst, (0, e_pad), constant_values=1 << 20).reshape(-1, P).T,
        "edges": _np.pad(feats, ((0, e_pad), (0, 0))).reshape(-1, P, feats.shape[1]).transpose(1, 0, 2),
    }
    for layer in range(2):
        for kind in "nsi":
            lay[f"w{kind}{layer}"] = _np.asarray(inputs[f"L0_gnn_W{kind}{layer}"]).T

    nc = _bacc.Bacc("TRN2", target_bir_lowering=False, num_devices=1)
    arrays, args = {}, []
    for name in _ORDER:
        a = _np.ascontiguousarray(lay[name])
        arrays[f"in_{name}_dram"] = a
        args.append(nc.dram_tensor(f"in_{name}_dram", a.shape, _mybir.dt.from_np(a.dtype), kind="ExternalInput").ap())
    args.append(nc.dram_tensor("out_0_dram", x.shape, _mybir.dt.float32, kind="ExternalOutput").ap())
    gnn_resnorm_kernel(nc, *args)
    r = _run(nc, [arrays], core_ids=[0])
    return r.results[0]["out_0_dram"]
```

```python
import concourse.bass as bass
from concourse import mybir
from contextlib import ExitStack


def gnn_resnorm_kernel(nc, x_rows, x_cols, src, dst, edges, wn0, ws0, wi0, wn1, ws1, wi1, out):
    f32, i32, bf16 = mybir.dt.float32, mybir.dt.int32, mybir.dt.bfloat16
    ALU, ACT, AX = mybir.AluOpType, mybir.ActivationFunctionType, mybir.AxisListType
    EPS = 1e-5
    SLOPE = (1.0 / 8.0 + 1.0 / 3.0) / 2.0

    P = 128
    D = x_rows.shape[1]
    N = out.shape[0]
    TILES = x_rows.shape[0] // P
    NP = TILES * P
    CHUNKS = src.shape[1]
    SUB = 4
    SLOTS = 4
    GC = SUB * SLOTS
    GROUPS = CHUNKS // GC
    W = 64
    WINDOWS = NP // W
    TAIL = N - (TILES - 1) * P
    assert GROUPS == TILES and CHUNKS % GC == 0

    PARTS = 3
    CUT = 7
    assert TILES % CUT == 0

    x_parts_rows = nc.dram_tensor("x_parts_rows", (NP, PARTS * D), bf16, kind="Internal").ap()
    h_parts_rows = nc.dram_tensor("h_parts_rows", (NP, PARTS * D), bf16, kind="Internal").ap()

    ctx = ExitStack()
    with ctx:
        def sb(name, shape, dt=f32):
            return ctx.enter_context(nc.sbuf_tensor(name, shape, dt))

        def sem(name):
            return ctx.enter_context(nc.semaphore(name))

        src_idx = sb("src_idx", [P, CHUNKS + GC], i32)
        dst_idx = sb("dst_idx", [P, CHUNKS + GC], i32)
        dst_f = sb("dst_f", [P, CHUNKS + GC])
        rel = sb("rel", [P, CHUNKS + GC])
        first_dst = sb("first_dst", [P, CHUNKS])
        bad_a = sb("bad_a", [P, CHUNKS])
        bad_b = sb("bad_b", [P, CHUNKS])
        bad_sum = sb("bad_sum", [P, 1])
        base_f = sb("base_f", [1, GROUPS * SLOTS])
        base_i = sb("base_i", [1, GROUPS * SLOTS], i32)
        general = sb("general", [1, 1], i32)
        ones = sb("ones", [P, P])
        ones_b = sb("ones_b", [P, P], bf16)
        zeros = sb("zeros", [P, P])
        column = sb("column", [P, W], bf16)
        lane = sb("lane", [P, P])
        ident = sb("ident", [P, P])

        EDGE, ROW, DEG = range(3)
        sums = sb("sums", [P, 3, NP])
        h_cols = sb("h_cols", [P, NP])

        idx = sb("idx", [P, GC], i32)
        rows = sb("rows", [P, GC, PARTS * D], bf16)
        feats = sb("feats", [P, GC, D])
        feats_rest = sb("feats_rest", [P, GC, D])
        feats_last = sb("feats_last", [P, GC, D], bf16)
        onehot = sb("onehot", [P, GC, W], bf16)
        x_stage = sums[:, DEG, :].rearrange("p (t d) -> p t d", t=TILES)
        x_parts = sb("x_parts", [P, TILES, PARTS, D], bf16)
        rel_w = sb("rel_w", [P, GC])

        wts = sb("wts", [P, 6, D])
        agg = sb("agg", [P, P])
        agg_mean = sb("agg_mean", [P, P])
        deg_1 = sb("deg_1", [P, P])
        deg_r = sb("deg_r", [P, P])
        iso = sb("iso", [P, P])
        h_iso = sb("h_iso", [P, P])
        h_con = sb("h_con", [P, P])
        leaked = sb("leaked", [P, D])
        h_row = sb("h_row", [P, D])
        h_rest = sb("h_rest", [P, D])
        h_parts = sb("h_parts", [P, PARTS, D], bf16)
        x_tile = sb("x_tile", [P, D])
        res = sb("res", [P, D])
        stats = sb("stats", [P, 6])
        mv = sb("mv", [P, 2])
        std = sb("std", [P, 1])
        rstd = sb("rstd", [P, 1])
        eps = sb("eps", [P, 1])
        y_row = sb("y_row", [P, D])

        ps_win = [ctx.enter_context(nc.psum_tensor(f"ps_win{i}", [P, 512], f32)) for i in range(2)]
        ps_node = ctx.enter_context(nc.psum_tensor("ps_node", [P, 512], f32))
        ps_t = ctx.enter_context(nc.psum_tensor("ps_t", [P, 512], f32))
        ps_set = ctx.enter_context(nc.psum_tensor("ps_set", [P, 512], f32))

        in_loaded = sem("in_loaded")
        tables_made = sem("tables_made")
        setup_step = sem("setup_step")
        bases_spread = sem("bases_spread")
        bad_counted = sem("bad_counted")
        setup_done = sem("setup_done")
        degrees_cleared = sem("degrees_cleared")
        idx_ready = sem("idx_ready")
        onehot_ready = sem("onehot_ready")
        rows_gathered = [sem(f"rows_gathered{j}") for j in range(SLOTS)]
        feats_loaded = [sem(f"feats_loaded{j}") for j in range(SLOTS)]
        rest_made = sem("rest_made")
        feats_cut = sem("feats_cut")
        x_staged = [sem(f"x_staged{i}") for i in range(TILES // CUT)]
        x_part = [sem(f"x_part{i}") for i in range(PARTS)]
        x_rest = sem("x_rest")
        x_parts_stored = sem("x_parts_stored")
        h_part = [sem(f"h_part{i}") for i in range(PARTS)]
        h_rest_made = sem("h_rest_made")
        window_summed = sem("window_summed")
        window_added = sem("window_added")
        pool_step = sem("pool_step")
        pe_step = sem("pe_step")
        dve_step = sem("dve_step")
        rel_ready = sem("rel_ready")
        agg_summed = sem("agg_summed")
        sums_cleared = sem("sums_cleared")
        deg_clamped = sem("deg_clamped")
        deg_inverted = sem("deg_inverted")
        iso_split = sem("iso_split")
        node_in = sem("node_in")
        node_out = sem("node_out")
        leak_made = sem("leak_made")
        h_made = sem("h_made")
        h_turned = sem("h_turned")
        h_kept = sem("h_kept")
        h_stored = sem("h_stored")
        x_loaded = sem("x_loaded")
        res_made = sem("res_made")
        stats_made = sem("stats_made")
        mv_made = sem("mv_made")
        std_made = sem("std_made")
        rstd_made = sem("rstd_made")
        y_made = sem("y_made")
        out_stored = sem("out_stored")

        block = ctx.enter_context(nc.Block())

        def upper(t):
            if len(t.shape) == 2:
                return t.bitcast(bf16).rearrange("p (d two) -> p d two", two=2)[:, :, 1]
            return t.bitcast(bf16).rearrange("p c (d two) -> p c d two", two=2)[:, :, :, 1]

        def at(v, n=1):
            return bass.ds(v, n)

        def load_flag(engine):
            return nc.values_load(general[0:1, 0:1], engines=(engine,), min_val=0, max_val=1)

        N_IN = 10

        @block.sync
        def _(sp):
            for i in range(TILES // CUT):
                sp.dma_start(x_stage[:, CUT * i:CUT * (i + 1), :],
                             x_rows[P * CUT * i:P * CUT * (i + 1), :].rearrange("(t p) d -> p t d", p=P)
                             ).then_inc(x_staged[i], 16)
            sp.dma_start(dst_idx[:, 0:CHUNKS], dst[:, :]).then_inc(in_loaded, 16)
            sp.dma_start(dst_idx[:, CHUNKS:], dst[:, 0:GC]).then_inc(in_loaded, 16)
            sp.dma_start(src_idx[:, 0:CHUNKS], src[:, :]).then_inc(in_loaded, 16)
            sp.dma_start(src_idx[:, CHUNKS:], src[:, 0:GC]).then_inc(in_loaded, 16)
            for k, w in enumerate((wn0, ws0, wi0, wn1, ws1, wi1)):
                sp.dma_start(wts[:, k, :], w[:, :]).then_inc(in_loaded, 16)
            sp.dma_start(h_cols[:, :], x_cols[:, :]).then_inc(in_loaded, 16)

            def load_feats(g, j):
                sp.dma_start(feats[:, SUB * j:SUB * (j + 1), :],
                             edges[:, at(g * GC + SUB * j, SUB), :]).then_inc(feats_loaded[j], 16)

            def load_x(t):
                if not isinstance(t, int) or t > 0:
                    sp.wait_ge(res_made, t)
                sp.dma_start(x_tile[:, :], x_rows[at(t * P, P), :]).then_inc(x_loaded, 16)

            for i in range(TILES // CUT):
                sp.wait_ge(x_part[1], i + 1)
                sp.wait_ge(x_part[2], i + 1)
                sp.dma_start(x_parts_rows[P * CUT * i:P * CUT * (i + 1), :].rearrange("(t p) d -> p t d", p=P),
                             x_parts[:, CUT * i:CUT * (i + 1), :, :].rearrange("p t k d -> p t (k d)")
                             ).then_inc(x_parts_stored, 16)
            sp.wait_ge(setup_done, 1)
            flag = load_flag(mybir.EngineType.SP)
            with sp.If(flag == 0):
                for j in range(SLOTS):
                    load_feats(0, j)
                with sp.Fori(1, GROUPS) as g:
                    for j in range(SLOTS):
                        sp.wait_ge(window_summed, (g - 1) * SLOTS + j + 1)
                        load_feats(g, j)
            with sp.Else():
                for j in range(SLOTS):
                    load_feats(0, j)
                with sp.Fori(1, GROUPS) as g:
                    sp.wait_ge(window_summed, g * WINDOWS + 1)
                    for j in range(SLOTS):
                        load_feats(g, j)
            load_x(0)
            with sp.Fori(1, TILES) as t:
                load_x(t)

        @block.gpsimd
        def _(pool):
            nc.gpsimd.iota(column[:, :], [[1, W]], base=0, channel_multiplier=0,
                           allow_small_or_imprecise_dtypes=True).then_inc(tables_made, 1)
            nc.gpsimd.iota(first_dst[:, :], [[P, GROUPS], [0, GC]], base=-P, channel_multiplier=0,
                           allow_small_or_imprecise_dtypes=True).then_inc(tables_made, 1)
            nc.gpsimd.iota(lane[:, :], [[1, P]], base=0, channel_multiplier=-1,
                           allow_small_or_imprecise_dtypes=True).then_inc(tables_made, 1)

            def gather(table, layer_groups, g, j):
                pool.wait_ge(idx_ready, (layer_groups + g) * SLOTS + j + 1)
                pool.sem_inc(pool_step, 1)
                for c in range(SUB * j, SUB * (j + 1)):
                    nc.gpsimd.indirect_dma_start(
                        rows[:, c, :], None, table[:, :],
                        bass.IndirectOffsetOnAxis(ap=idx[:, c:c + 1], axis=0)).then_inc(rows_gathered[j], 16)

            for layer, table in enumerate((x_parts_rows, h_parts_rows)):
                if layer == 0:
                    pool.wait_ge(x_parts_stored, 16 * (TILES // CUT))
                    pool.sem_inc(pool_step, 1)
                else:
                    pool.wait_ge(h_stored, 16 * TILES)
                    pool.sem_inc(pool_step, 1)
                with pool.Fori(0, GROUPS) as g:
                    for j in range(SLOTS):
                        gather(table, layer * GROUPS, g, j)

        @block.vector
        def _(dve):
            nc.vector.memset(ones[:, :], 1.0)
            nc.vector.memset(eps[:, :], EPS)
            nc.vector.memset(zeros[:, :], 0.0)
            nc.vector.memset(sums[:, EDGE:DEG, :], 0.0).then_inc(setup_step, 1)
            nc.vector.memset(ones_b[:, :], 1.0)
            for i in range(TILES // CUT + 1):
                if i < TILES // CUT:
                    t = slice(CUT * i, CUT * (i + 1))
                    dve.wait_ge(x_part[0], i + 1)
                    nc.vector.tensor_tensor(x_stage[:, t, :], x_stage[:, t, :], x_parts[:, t, 0, :],
                                            ALU.subtract).then_inc(x_rest, 1)
                if i:
                    t = slice(CUT * (i - 1), CUT * i)
                    dve.wait_ge(x_part[1], i)
                    nc.vector.tensor_tensor(x_parts[:, t, 2, :], x_stage[:, t, :], x_parts[:, t, 1, :],
                                            ALU.subtract).then_inc(x_part[2], 1)
            dve.wait_ge(x_part[2], TILES // CUT)
            nc.vector.memset(sums[:, DEG, :], 0.0).then_inc(degrees_cleared, 1)
            dve.wait_ge(degrees_cleared, 1)
            dve.wait_ge(in_loaded, 16 * (N_IN + 1))
            nc.vector.tensor_copy(dst_f[:, :], dst_idx[:, :]).then_inc(setup_step, 1)
            dve.wait_ge(tables_made, 3)
            nc.vector.tensor_single_scalar(ident[:, :], lane[:, :], 0.0, ALU.is_equal).then_inc(setup_step, 1)
            dve.wait_ge(setup_step, 2)
            nc.vector.tensor_scalar(base_f[0:1, :],
                                    dst_f[0:1, 0:CHUNKS].rearrange("p (s c) -> p s c", c=SUB)[:, :, 0],
                                    float(NP - W), None, ALU.min).then_inc(setup_step, 1)
            dve.wait_ge(setup_step, 4)
            nc.vector.tensor_copy(base_i[0:1, :], base_f[0:1, :]).then_inc(setup_step, 1)
            dve.wait_ge(bases_spread, 1)
            NB = GROUPS * SLOTS
            nc.vector.tensor_tensor(rel[:, 0:CHUNKS].rearrange("p (s c) -> p s c", c=SUB),
                                    dst_f[:, 0:CHUNKS].rearrange("p (s c) -> p s c", c=SUB),
                                    ps_set[:, 0:NB].unsqueeze(2).to_broadcast([P, NB, SUB]),
                                    ALU.subtract).then_inc(setup_step, 1)
            nc.vector.tensor_single_scalar(bad_a[:, :], dst_f[:, 0:CHUNKS], float(N), ALU.is_lt).then_inc(setup_step, 1)
            dve.wait_ge(setup_step, 7)
            nc.vector.tensor_copy(rel[:, CHUNKS:], rel[:, 0:GC]).then_inc(setup_step, 1)
            nc.vector.scalar_tensor_tensor(bad_b[:, :], rel[:, 0:CHUNKS], float(W), bad_a[:, :],
                                           ALU.is_ge, ALU.mult).then_inc(setup_step, 1)
            dve.wait_ge(setup_step, 9)
            nc.vector.scalar_tensor_tensor(bad_a[:, :], rel[:, 0:CHUNKS], 0.0, bad_b[:, :],
                                           ALU.is_lt, ALU.add).then_inc(setup_step, 1)
            dve.wait_ge(setup_step, 10)
            nc.vector.tensor_tensor(bad_b[:, :], dst_f[:, 0:CHUNKS], first_dst[:, :], ALU.is_lt).then_inc(setup_step, 1)
            dve.wait_ge(setup_step, 11)
            nc.vector.tensor_tensor(first_dst[:, :], bad_a[:, :], bad_b[:, :], ALU.max).then_inc(setup_step, 1)
            dve.wait_ge(setup_step, 12)
            nc.vector.reduce_max(bad_sum[:, :], first_dst[:, :], AX.X).then_inc(setup_step, 1)
            dve.wait_ge(bad_counted, 1)
            nc.vector.tensor_scalar(general[0:1, 0:1], ps_set[0:1, 256:257], 1.0, None, ALU.min).then_inc(setup_done, 1)

            def prepare(groups_before, g, j):
                nc.vector.tensor_copy(idx[:, SUB * j:SUB * (j + 1)],
                                      src_idx[:, at(g * GC + SUB * j, SUB)]).then_inc(idx_ready, 1)
                for c in range(SUB):
                    k = SUB * j + c
                    last = nc.vector.tensor_scalar(onehot[:, k, :], column[:, :], rel[:, at(g * GC + k)],
                                                   None, ALU.is_equal)
                last.then_inc(onehot_ready, 1)

            def cut_feats(g, j):
                c = slice(SUB * j, SUB * (j + 1))
                dve.wait_ge(feats_loaded[j], 16 * (g + 1))
                nc.vector.tensor_tensor(feats_rest[:, c, :], feats[:, c, :], upper(feats[:, c, :]),
                                        ALU.subtract).then_inc(rest_made, 1)
                dve.wait_ge(rest_made, g * SLOTS + j + 1)
                nc.vector.tensor_tensor(feats_last[:, c, :], feats_rest[:, c, :], upper(feats_rest[:, c, :]),
                                        ALU.subtract).then_inc(feats_cut, 1)

            def add_window(layer, at_node, ps):
                what = (slice(0, 3), 3) if layer == 0 else (slice(ROW, ROW + 1), 1)
                s = sums[:, what[0], at(at_node, W)]
                p = ps[:, what[0].start * W:what[0].stop * W].rearrange("p (k w) -> p k w", w=W)
                return nc.vector.tensor_tensor(s, s, p, ALU.add)

            def node_inputs(layer, t):
                n = layer * TILES + t
                tile = at(t * P, P)
                deg = sums[:, DEG, tile]
                if layer or not isinstance(t, int) or t > 0:
                    dve.wait_ge(node_out, n)
                nc.vector.tensor_tensor(agg[:, :], sums[:, EDGE, tile], sums[:, ROW, tile],
                                        ALU.add).then_inc(agg_summed, 1)
                nc.vector.tensor_scalar_max(deg_1[:, :], deg, 1.0).then_inc(deg_clamped, 1)
                nc.vector.tensor_single_scalar(iso[:, :], deg, 0.0, ALU.is_equal).then_inc(iso_split, 1)
                dve.wait_ge(deg_clamped, n + 1)
                nc.vector.reciprocal(deg_r[:, :], deg_1[:, :]).then_inc(deg_inverted, 1)
                dve.wait_ge(iso_split, 2 * n + 1)
                if layer:
                    dve.wait_ge(h_kept, TILES)
                nc.vector.tensor_tensor(h_iso[:, :], h_cols[:, tile], iso[:, :], ALU.mult).then_inc(iso_split, 1)
                dve.wait_ge(deg_inverted, n + 1)
                nc.vector.tensor_tensor(agg_mean[:, :], agg[:, :], deg_r[:, :], ALU.mult).then_inc(node_in, 1)
                dve.wait_ge(iso_split, 2 * n + 2)
                nc.vector.tensor_tensor(h_con[:, :], h_cols[:, tile], h_iso[:, :], ALU.subtract).then_inc(node_in, 1)
                if layer == 0:
                    dve.wait_ge(agg_summed, n + 1)
                    nc.vector.tensor_tensor(sums[:, ROW, tile], zeros[:, :], zeros[:, :], ALU.add).then_inc(sums_cleared, 1)

            def activate(layer, t):
                n = layer * TILES + t
                if layer == 0 and (not isinstance(t, int) or t > 0):
                    dve.wait_ge(h_part[0], t)
                    dve.wait_ge(h_rest_made, t)
                    dve.wait_ge(h_turned, t)
                elif layer and isinstance(t, int) and t == 0:
                    dve.wait_ge(h_part[0], TILES)
                    dve.wait_ge(h_rest_made, TILES)
                    dve.wait_ge(h_turned, TILES)
                elif layer:
                    dve.wait_ge(res_made, t)
                dve.wait_ge(leak_made, n + 1)
                nc.vector.tensor_tensor(h_row[:, :], ps_node[:, 0:D], leaked[:, :], ALU.max).then_inc(h_made, 1)

            def cut_h(t):
                dve.wait_ge(h_made, t + 1)
                if not isinstance(t, int) or t > 0:
                    dve.wait_ge(h_part[1], t)
                    dve.wait_ge(h_part[2], t)
                nc.vector.tensor_tensor(h_rest[:, :], h_row[:, :], upper(h_row[:, :]),
                                        ALU.subtract).then_inc(h_rest_made, 1)
                dve.wait_ge(h_rest_made, t + 1)
                if not isinstance(t, int) or t > 0:
                    dve.wait_ge(h_stored, 16 * t)
                nc.vector.tensor_tensor(h_parts[:, 2, :], h_rest[:, :], upper(h_rest[:, :]),
                                        ALU.subtract).then_inc(h_part[2], 1)

            def finish(t):
                dve.wait_ge(h_made, TILES + t + 1)
                dve.wait_ge(x_loaded, 16 * (t + 1))
                nc.vector.tensor_tensor(res[:, :], h_row[:, :], x_tile[:, :], ALU.add).then_inc(res_made, 1)
                dve.wait_ge(res_made, t + 1)
                nc.vector.bn_stats(stats[:, :], res[:, :]).then_inc(stats_made, 1)
                dve.wait_ge(stats_made, t + 1)
                dve.sem_inc(dve_step, 1)
                nc.vector.bn_aggr(mv[:, :], stats[:, :]).then_inc(mv_made, 1)
                dve.wait_ge(std_made, t + 1)
                nc.vector.reciprocal(rstd[:, :], std[:, :]).then_inc(rstd_made, 1)
                dve.wait_ge(rstd_made, t + 1)
                if not isinstance(t, int) or t > 0:
                    dve.wait_ge(out_stored, 16 * t)
                nc.vector.tensor_scalar(y_row[:, :], res[:, :], mv[:, 0:1], rstd[:, :],
                                        ALU.subtract, ALU.mult).then_inc(y_made, 1)

            def ordered_group(layer, g, last=False):
                bases = nc.values_load_multi_w_load_instructions(
                    base_i[0:1, at(g * SLOTS, SLOTS)], (mybir.EngineType.DVE,), min_val=0, max_val=NP - W,
                    skip_runtime_bounds_check_because="the setup keeps the bases within 0 .. NP - W")[1]
                for j in range(SLOTS):
                    n = (layer * GROUPS + g) * SLOTS + j
                    dve.wait_ge(window_summed, n + 1)
                    if layer or not (isinstance(g, int) and g == 0 and j == 0):
                        dve.wait_ge(window_added, n)
                    add_window(layer, bases[j], ps_win[j % 2]).then_inc(window_added, 1)
                    prepare(layer * GROUPS, g + 1, j)
                    if layer == 0 and j == 0:
                        cut_feats(g, SLOTS - 1)
                    elif layer == 0 and not last:
                        cut_feats(g + 1, j - 1)

            def tried_group(layer, g):
                before = (layer * GROUPS + g) * WINDOWS
                dve.wait_ge(window_summed, before + 1)
                dve.wait_ge(rel_ready, before + layer * GROUPS + g + 1)
                if layer == 0:
                    for j in range(SLOTS):
                        cut_feats(g, j)
                nc.vector.tensor_copy(idx[:, :], src_idx[:, at(g * GC, GC)]).then_inc(idx_ready, SLOTS)
                nc.vector.tensor_copy(rel_w[:, :], dst_f[:, at(g * GC, GC)]).then_inc(rel_ready, 1)
                with dve.Fori(0, WINDOWS) as w:
                    n = before + w
                    dve.wait_ge(window_summed, n + 1)
                    dve.wait_ge(rel_ready, n + layer * GROUPS + g + 2)
                    for k in range(GC):
                        last = nc.vector.tensor_scalar(onehot[:, k, :], column[:, :], rel_w[:, k:k + 1],
                                                       None, ALU.is_equal)
                    last.then_inc(onehot_ready, 1)
                    dve.wait_ge(onehot_ready, n + 1)
                    nc.vector.tensor_scalar(rel_w[:, :], rel_w[:, :], float(W), None,
                                            ALU.subtract).then_inc(rel_ready, 1)
                    dve.wait_ge(window_summed, n + 2)
                    add_window(layer, w * W, ps_win[0]).then_inc(window_added, 1)

            def node_tile(layer, t):
                node_inputs(layer, t)
                activate(layer, t)
                if layer == 0:
                    cut_h(t)
                else:
                    finish(t)

            dve.wait_ge(setup_done, 1)
            flag = load_flag(mybir.EngineType.DVE)
            with dve.If(flag == 0):
                for j in range(SLOTS):
                    prepare(0, 0, j)
                for j in range(SLOTS - 1):
                    cut_feats(0, j)
                for layer in range(2):
                    ordered_group(layer, 0)
                    with dve.Fori(1, GROUPS - 1) as g:
                        ordered_group(layer, g)
                        dve.wait_ge(window_added, (layer * GROUPS + g + 1) * SLOTS)
                        node_tile(layer, g - 1)
                    ordered_group(layer, GROUPS - 1, last=True)
                    dve.wait_ge(window_added, (layer + 1) * GROUPS * SLOTS)
                    node_tile(layer, TILES - 2)
                    node_tile(layer, TILES - 1)
            with dve.Else():
                dve.sem_inc(window_summed, 1)
                dve.sem_inc(window_added, 1)
                dve.sem_inc(rel_ready, 1)
                for layer in range(2):
                    with dve.Fori(0, GROUPS) as g:
                        tried_group(layer, g)
                    dve.wait_ge(window_added, (layer + 1) * GROUPS * WINDOWS + 1)
                    node_tile(layer, 0)
                    with dve.Fori(1, TILES) as t:
                        node_tile(layer, t)
                    if layer == 0:
                        dve.wait_ge(sums_cleared, TILES)

        @block.scalar
        def _(act):
            def leak(layer, t):
                n = layer * TILES + t
                act.wait_ge(node_out, n + 1)
                if layer or not isinstance(t, int) or t > 0:
                    act.wait_ge(h_made, n)
                nc.scalar.mul(leaked[:, :], ps_node[:, 0:D], SLOPE).then_inc(leak_made, 1)

            def keep(t):
                act.wait_ge(h_made, t + 1)
                if not isinstance(t, int) or t > 0:
                    act.wait_ge(h_stored, 16 * t)
                nc.scalar.copy(h_parts[:, 0, :], upper(h_row[:, :])).then_inc(h_part[0], 1)
                act.wait_ge(h_rest_made, t + 1)
                nc.scalar.copy(h_parts[:, 1, :], upper(h_rest[:, :])).then_inc(h_part[1], 1)
                act.wait_ge(h_part[0], t + 1)
                act.wait_ge(h_part[1], t + 1)
                act.wait_ge(h_part[2], t + 1)
                act.dma_start(h_parts_rows[at(t * P, P), :],
                              h_parts[:, :, :].rearrange("p k d -> p (k d)")).then_inc(h_stored, 16)
                act.wait_ge(h_turned, t + 1)
                nc.scalar.copy(h_cols[:, at(t * P, P)], ps_t[:, 0:P]).then_inc(h_kept, 1)

            def root(t):
                act.wait_ge(mv_made, t + 1)
                nc.scalar.activation(std[:, :], mv[:, 1:2], ACT.Sqrt, bias=eps[:, :]).then_inc(std_made, 1)

            def store(t, n):
                act.wait_ge(y_made, t + 1)
                act.dma_start(out[at(t * P, n), :], y_row[0:n, :]).then_inc(out_stored, 16)

            for i in range(TILES // CUT):
                t = slice(CUT * i, CUT * (i + 1))
                act.wait_ge(x_staged[i], 16)
                nc.scalar.copy(x_parts[:, t, 0, :], upper(x_stage[:, t, :])).then_inc(x_part[0], 1)
                act.wait_ge(x_rest, i + 1)
                nc.scalar.copy(x_parts[:, t, 1, :], upper(x_stage[:, t, :])).then_inc(x_part[1], 1)
            leak(0, 0)
            keep(0)
            with act.Fori(1, TILES) as t:
                leak(0, t)
                keep(t)
            act.wait_ge(h_stored, 16 * TILES)
            leak(1, 0)
            root(0)
            store(0, P)
            with act.Fori(1, TILES - 1) as t:
                leak(1, t)
                root(t)
                store(t, P)
            leak(1, TILES - 1)
            root(TILES - 1)
            store(TILES - 1, TAIL)
            act.wait_ge(out_stored, 16 * TILES)

        @block.tensor
        def _(pe):
            pe.wait_ge(setup_step, 4)
            nc.tensor.matmul(ps_set[:, 0:GROUPS * SLOTS], ones[0:1, :], base_f[0:1, :],
                             start=True, stop=True).then_inc(bases_spread, 1)
            pe.wait_ge(setup_step, 13)
            nc.tensor.matmul(ps_set[0:1, 256:257], bad_sum[:, :], ones[:, 0:1],
                             start=True, stop=True).then_inc(bad_counted, 1)

            def sum_chunks(layer, ps, ks):
                parts = {
                    EDGE: lambda k: [upper(feats[:, k, :]), upper(feats_rest[:, k, :]), feats_last[:, k, :]],
                    ROW: lambda k: [rows[:, k, i * D:(i + 1) * D] for i in range(PARTS)],
                    DEG: lambda k: [ones_b[:, :]],
                }
                for what, cut in parts.items():
                    if layer and what != ROW:
                        continue
                    lefts = [(left, k) for k in ks for left in cut(k)]
                    for i, (left, k) in enumerate(lefts):
                        last = nc.tensor.matmul(ps[:, what * W:(what + 1) * W], left, onehot[:, k, :],
                                                start=(i == 0), stop=(i == len(lefts) - 1))
                return last

            def ordered_group(layer, g):
                for j in range(SLOTS):
                    n = (layer * GROUPS + g) * SLOTS + j
                    pe.wait_ge(onehot_ready, n + 1)
                    if layer == 0:
                        pe.wait_ge(feats_cut, n + 1)
                    pe.wait_ge(rows_gathered[j], 16 * SUB * (layer * GROUPS + g + 1))
                    if layer or not (isinstance(g, int) and g == 0 and j < 2):
                        pe.wait_ge(window_added, n - 1)
                    sum_chunks(layer, ps_win[j % 2], range(SUB * j, SUB * (j + 1))).then_inc(window_summed, 1)

            def tried_group(layer, g):
                for j in range(SLOTS):
                    if layer == 0:
                        pe.wait_ge(feats_cut, g * SLOTS + j + 1)
                    pe.wait_ge(rows_gathered[j], 16 * SUB * (layer * GROUPS + g + 1))
                pe.sem_inc(pe_step, 1)
                with pe.Fori(0, WINDOWS) as w:
                    n = (layer * GROUPS + g) * WINDOWS + w
                    pe.wait_ge(onehot_ready, n + 1)
                    pe.wait_ge(window_added, n + 1)
                    sum_chunks(layer, ps_win[0], range(GC)).then_inc(window_summed, 1)

            def node_tile(layer, t):
                n = layer * TILES + t
                pe.wait_ge(node_in, 2 * (n + 1))
                if layer or not isinstance(t, int) or t > 0:
                    pe.wait_ge(h_made, n)
                for k, left in enumerate((agg_mean, h_con, h_iso)):
                    last = nc.tensor.matmul(ps_node[:, 0:D], left[:, :], wts[:, 3 * layer + k, :],
                                            start=(k == 0), stop=(k == 2))
                last.then_inc(node_out, 1)
                if layer == 0:
                    pe.wait_ge(h_made, t + 1)
                    if not isinstance(t, int) or t > 0:
                        pe.wait_ge(h_kept, t)
                    nc.tensor.transpose(ps_t[:, 0:P], h_row[:, :], ident[:, :]).then_inc(h_turned, 1)

            pe.wait_ge(setup_done, 1)
            flag = load_flag(mybir.EngineType.PE)
            with pe.If(flag == 0):
                for layer in range(2):
                    ordered_group(layer, 0)
                    with pe.Fori(1, GROUPS) as g:
                        ordered_group(layer, g)
                        node_tile(layer, g - 1)
                    node_tile(layer, TILES - 1)
            with pe.Else():
                for layer in range(2):
                    with pe.Fori(0, GROUPS) as g:
                        tried_group(layer, g)
                    node_tile(layer, 0)
                    with pe.Fori(1, TILES) as t:
                        node_tile(layer, t)


_ORDER = ["x_rows", "x_cols", "src", "dst", "edges", "wn0", "ws0", "wi0", "wn1", "ws1", "wi1"]


def kernel(**inputs):
    import numpy as _np
    import concourse.bacc as _bacc
    from concourse import mybir as _mybir
    from concourse.bass_utils import run_bass_kernel_spmd as _run

    x = _np.asarray(inputs["x"])
    src, dst = _np.asarray(inputs["src"]), _np.asarray(inputs["dst"])
    feats = _np.asarray(inputs["edge_attr_128"])
    P, GROUP = 128, 2048
    n, e = x.shape[0], src.shape[0]
    n_pad, e_pad = -n % P, -e % GROUP
    x_rows = _np.pad(x, ((0, n_pad), (0, 0)))
    lay = {
        "x_rows": x_rows,
        "x_cols": x_rows.T,
        "src": _np.pad(src, (0, e_pad)).reshape(-1, P).T,
        "dst": _np.pad(dst, (0, e_pad), constant_values=1 << 20).reshape(-1, P).T,
        "edges": _np.pad(feats, ((0, e_pad), (0, 0))).reshape(-1, P, feats.shape[1]).transpose(1, 0, 2),
    }
    for layer in range(2):
        for kind in "nsi":
            lay[f"w{kind}{layer}"] = _np.asarray(inputs[f"L0_gnn_W{kind}{layer}"]).T

    nc = _bacc.Bacc("TRN2", target_bir_lowering=False, num_devices=1)
    arrays, args = {}, []
    for name in _ORDER:
        a = _np.ascontiguousarray(lay[name])
        arrays[f"in_{name}_dram"] = a
        args.append(nc.dram_tensor(f"in_{name}_dram", a.shape, _mybir.dt.from_np(a.dtype), kind="ExternalInput").ap())
    args.append(nc.dram_tensor("out_0_dram", x.shape, _mybir.dt.float32, kind="ExternalOutput").ap())
    gnn_resnorm_kernel(nc, *args)
    r = _run(nc, [arrays], core_ids=[0])
    return r.results[0]["out_0_dram"]
```

```python
import concourse.bass as bass
from concourse import mybir
from contextlib import ExitStack


def gnn_resnorm_kernel(nc, x_rows, x_cols, src, dst, edges, wn0, ws0, wi0, wn1, ws1, wi1, out):
    f32, i32, i16 = mybir.dt.float32, mybir.dt.int32, mybir.dt.int16
    bf16, f16 = mybir.dt.bfloat16, mybir.dt.float16
    ALU, ACT, AX = mybir.AluOpType, mybir.ActivationFunctionType, mybir.AxisListType
    EPS = 1e-5
    SLOPE = (1.0 / 8.0 + 1.0 / 3.0) / 2.0

    P = 128
    D = x_rows.shape[1]
    N = out.shape[0]
    SRC_TILES = -(-N // P)
    COLS = x_rows.shape[0]
    TRIO = 3 * P
    TRIOS = COLS // TRIO
    CHUNKS = src.shape[1]
    SUB = 4
    SLOTS = 4
    GC = SUB * SLOTS
    GROUPS = CHUNKS // GC
    STEPS = GROUPS // 3
    SC = 3 * GC
    W = 64
    PAIRS = GC // 2
    WP = 24
    CODES = SRC_TILES * WP
    BANKS = 3
    PIECE = CODES // BANKS
    PARTS = 3
    CUT = 7
    CUTS = SRC_TILES // CUT
    RING = 3
    REST_RING = 2
    PAIR_RING = 4
    GENERAL = 2 * SUB
    TRIED = COLS // W
    ROUNDS = CHUNKS // GENERAL
    assert GROUPS == 3 * STEPS + 1 and TRIOS == STEPS + 1 and CODES % BANKS == 0 and SRC_TILES % CUT == 0
    assert COLS == TRIOS * TRIO and PIECE <= 512 and CHUNKS % GENERAL == 0

    ORDER = [("gather", SUB * j, j) for j in range(SLOTS)]
    for j in range(SLOTS):
        ORDER += [("count", GC + SUB * j, j), ("gather", 2 * GC + SUB * j, j)]
    SW = len(ORDER)
    LAST = ORDER[:SLOTS]
    COUNTED = {0: (0, 1), 1: (2, 3), 2: (4, 5), 3: (6, 7)}
    LAST_COUNTED = 3
    FEATS_CUT = (6, 7, 8, 9, 10, 11)
    PAIRS_ADDED = 0
    DEGREES_TAKEN = 4
    H_LOADED = 8
    WHEN = (dict(inputs=1, degrees=2, invert=3, products=3, activate=7, cut=8, turn=9),
            dict(inputs=1, products=2, invert=3, activate=4, statistics=5, normalize=6))
    LAST_WHEN = (dict(inputs=0, degrees=3, invert=3, products=3, activate=3, cut=3, turn=3),
                 dict(inputs=0, invert=1, products=1, activate=2, statistics=2, normalize=3))
    ALL_WINDOWS = GROUPS * SLOTS
    GATHERED = (2 * STEPS + 1) * SLOTS

    x_parts_rows = nc.dram_tensor("x_parts_rows", (COLS, PARTS * D), bf16, kind="Internal").ap()
    h_parts_rows = nc.dram_tensor("h_parts_rows", (COLS, PARTS * D), bf16, kind="Internal").ap()
    h_cols = nc.dram_tensor("h_cols", (P, COLS), f32, kind="Internal").ap()

    ctx = ExitStack()
    with ctx:
        def sb(name, shape, dt=f32):
            return ctx.enter_context(nc.sbuf_tensor(name, shape, dt))

        def sem(name):
            return ctx.enter_context(nc.semaphore(name))

        EDGE, ROW, DEG = range(3)
        sums = sb("sums", [P, 3, COLS])
        h_parts = sb("h_parts", [P, SRC_TILES, PARTS, D], bf16)
        counts = sb("counts", [P, PAIRS, CODES], bf16)

        tables = counts[:, :, :].rearrange("p a b -> p (a b)").bitcast(f32)
        TABLES = tables.shape[1] // CHUNKS
        dst_f, dst_raw, scratch_a, scratch_b, first_dst, src_raw = (
            tables[:, i * CHUNKS:(i + 1) * CHUNKS] for i in range(TABLES))
        src_idx = sb("src_idx", [P, CHUNKS], i16)
        rel = sb("rel", [P, (STEPS + 1) * SC], bf16)
        code = sb("code", [P, STEPS + 1, GC])
        lane = sb("lane", [P, STEPS + 1, GC])
        base_i = sb("base_i", [1, ALL_WINDOWS], i32)
        pair_i = sb("pair_i", [1, STEPS, PAIRS], i32)
        bad = sb("bad", [P, 1])
        general = sb("general", [1, 1], i32)
        ones = sb("ones", [P, P])
        zeros = sb("zeros", [P, TRIO], bf16)
        column = sb("column", [P, P], bf16)
        codes = sb("codes", [P, CODES], f16)
        ident = sb("ident", [P, P])

        idx = sb("idx", [P, 2, GC], i32)
        rows = sb("rows", [P, GC, PARTS * D], bf16)
        feats = sb("feats", [P, RING * SUB, D])
        base_f = feats[0:1, 0:2, :].rearrange("p c d -> p (c d)")[:, 0:ALL_WINDOWS]
        pair_f = feats[0:1, 2:4, :].rearrange("p c d -> p (c d)")[:, 0:STEPS * PAIRS].rearrange(
            "p (s q) -> p s q", q=PAIRS)
        onehot = {kind: sb(f"onehot_{kind}", [P, GC, W]) for kind in ("gather", "count")}
        is_code = sb("is_code", [P, PAIR_RING, 2, CODES], bf16)
        is_lane = sb("is_lane", [P, PAIR_RING, 2, P], bf16)
        own_hin, own_hcon, own_agg = (feats[:, SUB * i:SUB * i + 3, :].rearrange("p t d -> p (t d)") for i in (2, 1, 0))
        room = is_code[:, :, :, :].rearrange("p q c w -> p (q c w)").bitcast(f32)
        stages = [room[:, i * CUT * D:(i + 1) * CUT * D] for i in range(room.shape[1] // (CUT * D))]
        stages += [m[:, :, :].rearrange("p c w -> p (c w)")[:, 0:CUT * D] for m in onehot.values()]
        x_stage = [m.rearrange("p (t d) -> p t d", d=D) for m in stages[:CUTS]]
        assert len(x_stage) == CUTS
        rel_w = sb("rel_w", [P, GENERAL])

        feats_rest = sb("feats_rest", [P, REST_RING * SUB, D])
        wts = sb("wts", [P, 3, D])
        agg = sb("agg", [P, TRIO])
        deg_inv = sb("deg_inv", [P, TRIOS, 3])
        inv_now = sb("inv_now", [P, 2, 3])
        h_in = sb("h_in", [P, TRIO])
        h_con = sb("h_con", [P, TRIO])
        mean = sb("mean", [P, TRIO])
        total = mean
        h_row = sb("h_row", [P, TRIO])
        h_rest = sb("h_rest", [P, TRIO])
        res = h_rest
        row_parts = sb("row_parts", [P, 3, PARTS, D], bf16)
        turned = sb("turned", [P, TRIO])
        deg_row = turned[0:1, :]
        x_trio = turned
        stats = sb("stats", [P, 3, 6])
        mv = sb("mv", [P, 3, 2])
        std = sb("std", [P, 3])
        rstd = sb("rstd", [P, 3])
        eps = sb("eps", [P, 1])

        def bank(name, n=1):
            return ctx.enter_context(nc.psum_tensor(name, [P, n, 512], f32))

        ps_win = [bank(f"ps_win{i}") for i in range(2)]
        ps_count = bank("ps_count", BANKS)
        ps_dense = bank("ps_dense")
        ps_node = bank("ps_node")
        ps_self = bank("ps_self")

        def node_buffers(own):
            if own:
                return own_agg, own_hcon, own_hin, ps_win[0], ps_win[1]
            return agg[:, :], h_con[:, :], h_in[:, :], ps_node, ps_self

        dst_loaded = sem("dst_loaded")
        src_loaded = sem("src_loaded")
        wts_loaded = sem("wts_loaded")
        iotas_made = sem("iotas_made")
        setup_step = sem("setup_step")
        bases_spread = sem("bases_spread")
        pairs_spread = sem("pairs_spread")
        bad_counted = sem("bad_counted")
        setup_done = sem("setup_done")
        sums_zeroed = sem("sums_zeroed")
        x_staged = [sem(f"x_staged{i}") for i in range(CUTS)]
        x_part = [sem(f"x_part{i}") for i in range(PARTS)]
        x_rest = sem("x_rest")
        x_parts_stored = sem("x_parts_stored")
        parts_loaded = sem("parts_loaded")
        idx_ready = sem("idx_ready")
        onehot_ready = {kind: sem(f"onehot_{kind}_ready") for kind in ("gather", "count")}
        rows_gathered = [sem(f"rows_gathered{j}") for j in range(SLOTS)]
        feats_loaded = [sem(f"feats_loaded{j}") for j in range(RING)]
        rest_made = sem("rest_made")
        feats_cut = sem("feats_cut")
        window_summed = sem("window_summed")
        window_added = sem("window_added")
        codes_ready = sem("codes_ready")
        piece_counted = sem("piece_counted")
        piece_kept = sem("piece_kept")
        group_multiplied = sem("group_multiplied")
        pair_added = sem("pair_added")
        pool_step = sem("pool_step")
        dve_step = sem("dve_step")
        pe_step = sem("pe_step")
        act_step = sem("act_step")
        rel_ready = sem("rel_ready")
        h_loaded = sem("h_loaded")
        agg_summed = sem("agg_summed")
        con_made = sem("con_made")
        deg_taken = sem("deg_taken")
        deg_turned = sem("deg_turned")
        deg_clamped = sem("deg_clamped")
        deg_inverted = sem("deg_inverted")
        mean_made = sem("mean_made")
        total_made = sem("total_made")
        h_split = sem("h_split")
        node_in = sem("node_in")
        sums_cleared = sem("sums_cleared")
        node_out = sem("node_out")
        h_made = sem("h_made")
        part_copied = sem("part_copied")
        h_rest_made = sem("h_rest_made")
        last_part_made = sem("last_part_made")
        parts_stored = sem("parts_stored")
        h_turned = sem("h_turned")
        turned_kept = sem("turned_kept")
        turned_stored = sem("turned_stored")
        x_loaded = sem("x_loaded")
        res_made = sem("res_made")
        stats_made = sem("stats_made")
        mv_made = sem("mv_made")
        std_made = sem("std_made")
        rstd_made = sem("rstd_made")
        y_made = sem("y_made")
        out_stored = sem("out_stored")

        setup_marks = {}
        block = ctx.enter_context(nc.Block())

        def upper(t):
            if len(t.shape) == 2:
                return t.bitcast(bf16).rearrange("p (d two) -> p d two", two=2)[:, :, 1]
            return t.bitcast(bf16).rearrange("p c (d two) -> p c d two", two=2)[:, :, :, 1]

        def lower(t):
            return t.bitcast(bf16).rearrange("p c (d two) -> p c d two", two=2)[:, :, :, 0]

        def at(v, n=1):
            return bass.ds(v, n)

        def zero(v):
            return isinstance(v, int) and v == 0

        def load_flag(engine):
            return nc.values_load(general[0:1, 0:1], engines=(engine,), min_val=0, max_val=1)

        def by_tile(t):
            return t.rearrange("(t p) d -> p t d", p=P)

        def windows_before(layer, s):
            return s * SW if layer == 0 else ALL_WINDOWS + s * 2 * SLOTS

        def order(layer, s):
            if s is None:
                return LAST
            return [w for w in ORDER if layer == 0 or w[0] == "gather"]

        @block.sync
        def _(sp):
            def load_weights(layer):
                if layer:
                    sp.wait_ge(node_out, TRIOS)
                for k, w in enumerate(((wn0, ws0, wi0), (wn1, ws1, wi1))[layer]):
                    sp.dma_start(wts[:, k, :], w[:, :]).then_inc(wts_loaded, 16)

            sp.dma_start(dst_raw.bitcast(i32), dst[:, :]).then_inc(dst_loaded, 16)
            for i in range(CUTS):
                r = slice(P + P * CUT * i, P + P * CUT * (i + 1))
                sp.dma_start(x_stage[i], by_tile(x_rows[r, :])).then_inc(x_staged[i], 16)
            sp.dma_start(src_raw.bitcast(i32), src[:, :]).then_inc(src_loaded, 16)
            sp.wait_ge(setup_step, 1)
            for r in (0, P + SRC_TILES * P):
                sp.dma_start(x_parts_rows[r:r + P, :], zeros[:, :]).then_inc(x_parts_stored, 16)
            load_weights(0)
            for i in range(CUTS):
                r = slice(P + P * CUT * i, P + P * CUT * (i + 1))
                sp.wait_ge(x_part[0], i + 1)
                sp.wait_ge(x_part[1], i + 1)
                sp.wait_ge(x_part[2], i + 1)
                sp.dma_start(by_tile(x_parts_rows[r, :]),
                             h_parts[:, CUT * i:CUT * (i + 1), :, :].rearrange("p t k d -> p t (k d)")
                             ).then_inc(x_parts_stored, 16)

            def load_feats(chunk, slot, n=SUB):
                sp.dma_start(feats[:, SUB * slot:SUB * slot + n, :],
                             edges[:, at(chunk, n), :]).then_inc(feats_loaded[slot], 16)

            def load_h(layer, u):
                n = layer * TRIOS + u
                if not zero(n):
                    sp.wait_ge(node_out, n)
                sp.dma_start(h_in[:, :], (x_cols, h_cols)[layer][:, at(u * TRIO, TRIO)]).then_inc(h_loaded, 16)

            def load_last_h(layer):
                sp.wait_ge(window_summed, STEPS * SW + 3)
                sp.wait_ge(h_split, layer * TRIOS + TRIOS - 1)
                sp.dma_start(own_hin, (x_cols, h_cols)[layer][:, (TRIOS - 1) * TRIO:TRIOS * TRIO]).then_inc(h_loaded, 16)

            def load_x(u):
                if not zero(u):
                    sp.wait_ge(res_made, u)
                sp.dma_start(x_trio[:, :].rearrange("p (t d) -> p t d", d=D),
                             by_tile(x_rows[at(u * TRIO, TRIO), :])).then_inc(x_loaded, 16)

            def step(s):
                for k in range(SW):
                    sp.wait_ge(window_summed, s * SW + k + 1)
                    ahead, at_k = divmod(k + RING, SW)
                    load_feats((s + ahead) * SC + ORDER[at_k][1], at_k % RING)
                    if k == H_LOADED:
                        load_h(0, s)

            sp.wait_ge(setup_done, 1)
            flag = load_flag(mybir.EngineType.SP)
            with sp.If(flag == 0):
                for k in range(RING):
                    load_feats(ORDER[k][1], k)
                step(0)
                with sp.Fori(1, STEPS) as s:
                    step(s)
                sp.wait_ge(window_summed, STEPS * SW + 1)
                load_feats(STEPS * SC + LAST[3][1], 3 % RING)
                load_last_h(0)
                sp.wait_ge(group_multiplied, STEPS)
                sp.wait_ge(window_summed, STEPS * SW + SLOTS)
                for i in range(CUTS):
                    r = slice(P + P * CUT * i, P + P * CUT * (i + 1))
                    sp.wait_ge(parts_stored, 16 * min(-(-r.stop // TRIO), TRIOS))
                    sp.dma_start(h_parts[:, CUT * i:CUT * (i + 1), :, :].rearrange("p t k d -> p t (k d)"),
                                 by_tile(h_parts_rows[r, :])).then_inc(parts_loaded, 16)
                sp.wait_ge(turned_stored, 16 * TRIOS)
                load_weights(1)
                load_h(1, 0)
                load_x(0)
                with sp.Fori(1, TRIOS - 1) as u:
                    load_h(1, u)
                    load_x(u)
                load_last_h(1)
                load_x(TRIOS - 1)
            with sp.Else():
                with sp.Fori(0, ROUNDS) as r:
                    sp.wait_ge(window_summed, r * TRIED + 1)
                    for j in range(2):
                        load_feats(r * GENERAL + SUB * j, j)
                load_h(0, 0)
                with sp.Fori(1, TRIOS) as u:
                    load_h(0, u)
                sp.wait_ge(turned_stored, 16 * TRIOS)
                load_weights(1)
                load_h(1, 0)
                load_x(0)
                with sp.Fori(1, TRIOS) as u:
                    load_h(1, u)
                    load_x(u)

        @block.gpsimd
        def _(pool):
            nc.gpsimd.iota(column[:, :], [[1, P]], base=0, channel_multiplier=0,
                           allow_small_or_imprecise_dtypes=True).then_inc(iotas_made, 1)
            nc.gpsimd.iota(codes[:, :], [[1, CODES]], base=0, channel_multiplier=0,
                           allow_small_or_imprecise_dtypes=True).then_inc(iotas_made, 1)
            nc.gpsimd.iota(first_dst, [[P, GROUPS], [0, GC]], base=-P, channel_multiplier=0,
                           allow_small_or_imprecise_dtypes=True).then_inc(iotas_made, 1)
            nc.gpsimd.iota(agg[:, 0:P], [[1, P]], base=0, channel_multiplier=-1,
                           allow_small_or_imprecise_dtypes=True).then_inc(iotas_made, 1)
            nc.gpsimd.memset(sums[:, :, :], 0.0).then_inc(sums_zeroed, 1)

            def gather(table, half, j):
                pool.sem_inc(pool_step, 1)
                for c in range(SUB * j, SUB * (j + 1)):
                    nc.gpsimd.indirect_dma_start(
                        rows[:, c, :], None, table[:, :],
                        bass.IndirectOffsetOnAxis(ap=idx[:, half, c:c + 1], axis=0)).then_inc(rows_gathered[j], 16)

            def gather_group(layer, table, half, s, group):
                pool.wait_ge(idx_ready, group + 1)
                for j in range(SLOTS):
                    if half:
                        pool.wait_ge(window_summed, windows_before(layer, s) + j + 1)
                    elif not zero(s):
                        place = SLOTS + (2 * j + 1 if layer == 0 else j)
                        pool.wait_ge(window_summed, windows_before(layer, s - 1) + place + 1)
                    gather(table, half, j)

            def stored(layer):
                if layer == 0:
                    pool.wait_ge(x_parts_stored, 16 * (CUTS + 2))
                else:
                    pool.wait_ge(parts_stored, 16 * TRIOS)

            pool.wait_ge(setup_done, 1)
            flag = load_flag(mybir.EngineType.Pool)
            with pool.If(flag == 0):
                for layer, table in enumerate((x_parts_rows, h_parts_rows)):
                    stored(layer)
                    groups = layer * (2 * STEPS + 1)
                    gather_group(layer, table, 0, 0, groups)
                    with pool.Fori(0, STEPS) as s:
                        gather_group(layer, table, 1, s, groups + 2 * s + 1)
                        gather_group(layer, table, 0, s + 1, groups + 2 * s + 2)
            with pool.Else():
                for layer, table in enumerate((x_parts_rows, h_parts_rows)):
                    stored(layer)
                    with pool.Fori(0, ROUNDS) as r:
                        pool.wait_ge(idx_ready, layer * ROUNDS + r + 1)
                        for j in range(2):
                            gather(table, 0, j)

        @block.vector
        def _(dve):
            def setup(ins):
                ins.then_inc(setup_step, 1)
                done[0] += 1
                return done[0]

            done = [0]
            nc.vector.memset(ones[:, :], 1.0)
            nc.vector.memset(zeros[:, :], 0.0)
            nc.vector.memset(eps[:, :], EPS)
            setup(nc.vector.memset(rel[:, CHUNKS:], -1.0))
            dve.wait_ge(dst_loaded, 16)
            n_dst = setup(nc.vector.tensor_copy(dst_f, dst_raw.bitcast(i32)))
            dve.wait_ge(setup_step, n_dst)
            first = dst_f[0:1, :].rearrange("p (s c) -> p s c", c=SUB)[:, :, 0]
            setup(nc.vector.tensor_scalar(base_f[0:1, :], first, float(COLS - P - W), None, ALU.min))
            counted = dst_f[0:1, 0:STEPS * SC].rearrange("p (s c) -> p s c", c=SC)[:, :, GC:2 * GC]
            first = counted.rearrange("p s (q c) -> p s q c", c=2)[:, :, :, 0]
            n_bases = setup(nc.vector.tensor_scalar(pair_f[0:1, :, :], first, float(COLS - P - WP), None, ALU.min))
            dve.wait_ge(setup_step, n_bases)
            setup(nc.vector.tensor_scalar(base_i[0:1, :], base_f[0:1, :], float(P), None, ALU.add))
            setup(nc.vector.tensor_scalar(pair_i[0:1, :, :], pair_f[0:1, :, :], float(P), None, ALU.add))
            for i in range(CUTS + 1):
                if i < CUTS:
                    t = slice(CUT * i, CUT * (i + 1))
                    dve.wait_ge(x_part[0], i + 1)
                    nc.vector.tensor_tensor(x_stage[i], x_stage[i], h_parts[:, t, 0, :],
                                            ALU.subtract).then_inc(x_rest, 1)
                if i:
                    t = slice(CUT * (i - 1), CUT * i)
                    dve.wait_ge(x_part[1], i)
                    nc.vector.tensor_tensor(h_parts[:, t, 2, :], x_stage[i - 1], h_parts[:, t, 1, :],
                                            ALU.subtract).then_inc(x_part[2], 1)
            dve.wait_ge(iotas_made, 4)
            setup(nc.vector.tensor_single_scalar(ident[:, :], agg[:, 0:P], 0.0, ALU.is_equal))
            dve.wait_ge(bases_spread, 1)
            dst_w = dst_f.rearrange("p (s c) -> p s c", c=SUB)
            rel_f = scratch_a.rearrange("p (s c) -> p s c", c=SUB)
            setup(nc.vector.tensor_tensor(rel_f, dst_w,
                                          ps_node[:, 0, 0:ALL_WINDOWS].unsqueeze(2).to_broadcast([P, ALL_WINDOWS, SUB]),
                                          ALU.subtract))
            n = setup(nc.vector.tensor_single_scalar(scratch_b, dst_f, float(N), ALU.is_lt))
            dve.wait_ge(setup_step, n)
            setup(nc.vector.tensor_copy(rel[:, 0:CHUNKS], scratch_a))
            n = setup(nc.vector.scalar_tensor_tensor(dst_raw, scratch_a, float(W), scratch_b, ALU.is_ge, ALU.mult))
            dve.wait_ge(setup_step, n)
            n = setup(nc.vector.scalar_tensor_tensor(dst_raw, scratch_a, 0.0, dst_raw, ALU.is_lt, ALU.max))
            setup(nc.vector.tensor_tensor(scratch_b, dst_f, first_dst, ALU.is_lt))
            dve.wait_ge(setup_step, n + 1)
            setup(nc.vector.tensor_tensor(first_dst, dst_raw, scratch_b, ALU.max))
            dve.wait_ge(pairs_spread, 1)

            def of_counted(t):
                return t[:, 0:STEPS * SC].rearrange("p (s c) -> p s c", c=SC)[:, :, GC:2 * GC]

            def pairs(t):
                return t.rearrange("p s (q c) -> p s q c", c=2)

            PW = STEPS * PAIRS
            pair_base = ps_self[:, 0, 0:PW].unsqueeze(2).to_broadcast([P, PW, 2])
            rel_p = scratch_a[:, 0:STEPS * GC]
            n = setup(nc.vector.tensor_copy(rel_p.rearrange("p (s c) -> p s c", c=GC), of_counted(dst_f)))
            dve.wait_ge(setup_step, n)
            n = setup(nc.vector.tensor_tensor(rel_p.rearrange("p (q c) -> p q c", c=2),
                                              rel_p.rearrange("p (q c) -> p q c", c=2), pair_base, ALU.subtract))
            dve.wait_ge(setup_step, n)
            out_p = scratch_b[:, 0:STEPS * GC]
            n = setup(nc.vector.tensor_single_scalar(out_p, rel_p, float(WP), ALU.is_ge))
            dve.wait_ge(setup_step, n)
            n = setup(nc.vector.scalar_tensor_tensor(out_p, rel_p, 0.0, out_p, ALU.is_lt, ALU.max))
            dve.wait_ge(setup_step, n)
            n = setup(nc.vector.tensor_tensor(first_dst[:, 0:STEPS * GC], first_dst[:, 0:STEPS * GC], out_p, ALU.max))
            dve.wait_ge(setup_step, n)
            n_bad = setup(nc.vector.reduce_max(bad[:, :], first_dst, AX.X))
            dve.wait_ge(src_loaded, 16)
            src_i = src_raw.bitcast(i32)
            setup(nc.vector.tensor_scalar(src_idx[:, :], src_i, float(P), None, ALU.add))
            part_i = dst_raw.bitcast(i32)
            n = setup(nc.vector.tensor_single_scalar(part_i, src_i, 7, ALU.logical_shift_right))
            dve.wait_ge(setup_step, n)
            n = setup(nc.vector.tensor_copy(scratch_b, part_i))
            dve.wait_ge(setup_step, n)
            setup(nc.vector.tensor_single_scalar(part_i, src_i, P - 1, ALU.bitwise_and))
            n = setup(nc.vector.scalar_tensor_tensor(code[:, 0:STEPS, :], of_counted(scratch_b), float(WP),
                                                     rel_p.rearrange("p (s c) -> p s c", c=GC), ALU.mult, ALU.add))
            dve.wait_ge(setup_step, n)
            n = setup(nc.vector.tensor_copy(lane[:, 0:STEPS, :], of_counted(part_i)))
            dve.wait_ge(setup_step, n)
            setup(nc.vector.tensor_copy(code[:, STEPS, :], code[:, 0, :]))
            n = setup(nc.vector.tensor_copy(lane[:, STEPS, :], lane[:, 0, :]))
            dve.wait_ge(setup_step, n)
            setup_marks["bases"], setup_marks["bad"] = n_bases, n_bad
            dve.wait_ge(x_part[2], CUTS)
            dve.wait_ge(sums_zeroed, 1)
            dve.wait_ge(bad_counted, 1)
            nc.vector.tensor_scalar(general[0:1, 0:1], ps_node[0:1, 0, 256:257], 1.0, None, ALU.min).then_inc(setup_done, 1)

            def place_indices(chunk, half):
                nc.vector.tensor_copy(idx[:, half, :], src_idx[:, at(chunk, GC)]).then_inc(idx_ready, 1)

            def make_onehot(kind, chunk, j):
                nc.vector.tensor_tensor(onehot[kind][:, SUB * j:SUB * (j + 1), :],
                                        column[:, 0:W].unsqueeze(1).to_broadcast([P, SUB, W]),
                                        rel[:, at(chunk, SUB)].unsqueeze(2).to_broadcast([P, SUB, W]),
                                        ALU.is_equal).then_inc(onehot_ready[kind], 1)

            def make_pair(n, s, q):
                if not (isinstance(n, int) and n < PAIR_RING):
                    dve.wait_ge(piece_counted, (n - PAIR_RING + 1) * BANKS)
                i = q % PAIR_RING
                for c in range(2):
                    nc.vector.tensor_scalar(is_lane[:, i, c, :], column[:, :], lane[:, at(s), 2 * q + c],
                                            None, ALU.is_equal)
                for c in range(2):
                    last = nc.vector.tensor_scalar(is_code[:, i, c, :], codes[:, :], code[:, at(s), 2 * q + c],
                                                   None, ALU.is_equal)
                last.then_inc(codes_ready, 1)

            def cut_feats(s, k):
                i = FEATS_CUT.index(k)
                nth = s * len(FEATS_CUT) + i
                slot = k % RING
                f = feats[:, SUB * slot:SUB * (slot + 1), :]
                rest = feats_rest[:, SUB * (i % REST_RING):SUB * (i % REST_RING + 1), :]
                dve.wait_ge(feats_loaded[slot], 16 * (s * (SW // RING) + k // RING + 1))
                nc.vector.tensor_tensor(rest, f, upper(f), ALU.subtract).then_inc(rest_made, 1)
                dve.wait_ge(rest_made, nth + 1)
                nc.vector.tensor_tensor(lower(f), rest, upper(rest), ALU.subtract).then_inc(feats_cut, 1)

            def add_window(layer, kind, col, ps):
                if layer:
                    what = slice(ROW, ROW + 1)
                elif kind == "gather":
                    what = slice(EDGE, DEG + 1)
                else:
                    what = slice(EDGE, DEG + 1, 2)
                s = sums[:, what, at(col, W)]
                p = ps[:, 0, 0:3 * W].rearrange("p (k w) -> p k w", w=W)[:, what, :]
                return nc.vector.tensor_tensor(s, s, p, ALU.add)

            def node_inputs(layer, u, own=False):
                n = layer * TRIOS + u
                trio = at(u * TRIO, TRIO)
                deg = sums[:, DEG, trio]
                msg, con, iso, _, _ = node_buffers(own)
                if not (own or zero(n)):
                    dve.wait_ge(node_out, n)
                nc.vector.tensor_tensor(msg, sums[:, EDGE, trio], sums[:, ROW, trio],
                                        ALU.add).then_inc(agg_summed, 1)
                nc.vector.tensor_single_scalar(con, deg, 0.0, ALU.is_gt).then_inc(con_made, 1)
                dve.wait_ge(con_made, n + 1)
                dve.wait_ge(h_loaded, 16 * (n + 1))
                nc.vector.tensor_tensor(con, iso, con, ALU.mult).then_inc(h_split, 1)
                dve.wait_ge(h_split, n + 1)
                nc.vector.tensor_tensor(iso, iso, con, ALU.subtract).then_inc(node_in, 1)

            def invert(layer, u, own=False):
                n = layer * TRIOS + u
                inv = inv_now[:, int(own), :]
                if not (own or zero(n)):
                    dve.wait_ge(mean_made, 3 * n)
                if layer:
                    nc.vector.tensor_copy(inv, deg_inv[:, at(u), :]).then_inc(deg_inverted, 1)
                    return
                dve.wait_ge(deg_turned, u + 1)
                nc.vector.tensor_scalar_max(inv, node_buffers(own)[4][:, 0, TRIO:TRIO + 3], 1.0).then_inc(deg_clamped, 1)
                dve.wait_ge(deg_clamped, u + 1)
                nc.vector.reciprocal(inv, inv).then_inc(deg_inverted, 1)
                dve.wait_ge(deg_inverted, u + 1)
                nc.vector.tensor_tensor(deg_inv[:, at(u), :], inv, zeros[:, 0:3], ALU.add)

            def activate(layer, u, own=False):
                n = layer * TRIOS + u
                dve.wait_ge(mean_made, 3 * (n + 1))
                nc.vector.tensor_tensor(total[:, :], node_buffers(own)[4][:, 0, 0:TRIO], mean[:, :],
                                        ALU.add).then_inc(total_made, 1)
                if layer == 0 and not zero(u):
                    dve.wait_ge(part_copied, 2 * u)
                    dve.wait_ge(h_turned, u)
                elif layer and zero(u):
                    dve.wait_ge(part_copied, 2 * TRIOS)
                    dve.wait_ge(h_turned, TRIOS)
                dve.wait_ge(total_made, n + 1)
                nc.vector.scalar_tensor_tensor(h_row[:, :], total[:, :], SLOPE, total[:, :],
                                               ALU.mult, ALU.max).then_inc(h_made, 1)

            def cut_h(u):
                dve.wait_ge(h_made, u + 1)
                if not zero(u):
                    dve.wait_ge(last_part_made, u)
                nc.vector.tensor_tensor(h_rest[:, :], h_row[:, :], upper(h_row[:, :]),
                                        ALU.subtract).then_inc(h_rest_made, 1)
                dve.wait_ge(h_rest_made, u + 1)
                if not zero(u):
                    dve.wait_ge(parts_stored, 16 * u)
                nc.vector.tensor_tensor(row_parts[:, :, 2, :], h_rest[:, :].rearrange("p (t d) -> p t d", d=D),
                                        upper(h_rest[:, :]).rearrange("p (t d) -> p t d", d=D),
                                        ALU.subtract).then_inc(last_part_made, 1)

            def statistics(u):
                dve.wait_ge(h_made, TRIOS + u + 1)
                dve.wait_ge(x_loaded, 16 * (u + 1))
                if zero(u):
                    dve.wait_ge(last_part_made, TRIOS)
                else:
                    dve.wait_ge(out_stored, 16 * u)
                nc.vector.tensor_tensor(res[:, :], h_row[:, :], x_trio[:, :], ALU.add).then_inc(res_made, 1)
                dve.wait_ge(res_made, u + 1)
                for t in range(3):
                    nc.vector.bn_stats(stats[:, t, :], res[:, t * D:(t + 1) * D]).then_inc(stats_made, 1)
                dve.wait_ge(stats_made, 3 * (u + 1))
                dve.sem_inc(dve_step, 1)
                for t in range(3):
                    nc.vector.bn_aggr(mv[:, t, :], stats[:, t, :]).then_inc(mv_made, 1)

            def normalize(u):
                dve.wait_ge(std_made, u + 1)
                nc.vector.reciprocal(rstd[:, :], std[:, :]).then_inc(rstd_made, 1)
                dve.wait_ge(rstd_made, u + 1)
                dve.wait_ge(mv_made, 3 * (u + 1))
                for t in range(3):
                    r = res[:, t * D:(t + 1) * D]
                    nc.vector.tensor_scalar(r, r, mv[:, t, 0:1], rstd[:, t:t + 1],
                                            ALU.subtract, ALU.mult).then_inc(y_made, 1)

            def load_columns(table, first, n, most):
                return nc.values_load_multi_w_load_instructions(
                    table[0:1, at(first, n)], (mybir.EngineType.DVE,), min_val=P, max_val=most,
                    skip_runtime_bounds_check_because="the setup keeps the bases within the columns")[1]

            pair_base_of = pair_i[0:1, :, :].rearrange("o s q -> o (s q)")

            def add_pairs(layer, s):
                g = layer * STEPS + s
                cols = load_columns(pair_base_of, s * PAIRS, PAIRS, COLS - WP)
                dve.wait_ge(group_multiplied, g + 1)
                dve.wait_ge(window_added, windows_before(layer, s + 1) + PAIRS_ADDED + 1)
                for q in range(PAIRS):
                    r = sums[:, ROW, at(cols[q], WP)]
                    if not (zero(g) and q == 0):
                        dve.wait_ge(pair_added, g * PAIRS + q)
                    nc.vector.tensor_tensor(r, r, ps_dense[:, 0, q * WP:(q + 1) * WP],
                                            ALU.add).then_inc(pair_added, 1)

            def node_stage(layer, u, k, last):
                when = (LAST_WHEN if last else WHEN)[layer]
                if when["inputs"] == k:
                    dve.wait_ge(window_added, windows_before(layer, u + 1))
                    dve.wait_ge(pair_added, (layer * STEPS + u + 1) * PAIRS)
                    node_inputs(layer, u)
                if last and k == SLOTS - 1:
                    dve.wait_ge(window_added, windows_before(layer, STEPS) + SLOTS)
                    node_inputs(layer, TRIOS - 1, own=True)
                    invert(layer, TRIOS - 1, own=True)
                if when["activate"] == k:
                    activate(layer, u)
                if when.get("cut") == k:
                    cut_h(u)
                if when.get("statistics") == k:
                    statistics(u)
                if when.get("normalize") == k:
                    normalize(u)

            def step(layer, s, u=None, last=False):
                ws = order(layer, None if last else s)
                bases = load_columns(base_i, s * 3 * SLOTS, SLOTS if last else 3 * SLOTS, COLS - W)
                before = windows_before(layer, s)
                if not last:
                    place_indices(s * SC + 2 * GC, 1)
                for k, (kind, chunk, j) in enumerate(ws):
                    n = before + k
                    dve.wait_ge(window_summed, n + 1)
                    if not zero(n):
                        dve.wait_ge(window_added, n)
                    if u is not None and k == PAIRS_ADDED + 1:
                        dve.wait_ge(pair_added, (layer * STEPS + s) * PAIRS)
                    add_window(layer, kind, bases[chunk // SUB], ps_win[k % 2]).then_inc(window_added, 1)
                    if u is not None and k == (LAST_WHEN if last else WHEN)[layer]["invert"]:
                        invert(layer, u)
                    if kind == "count":
                        make_onehot(kind, (s + 1) * SC + chunk, j)
                    elif not last:
                        make_onehot(kind, s * SC + chunk + 2 * GC if chunk < GC else (s + 1) * SC + chunk - 2 * GC, j)
                    elif layer == 0:
                        make_onehot(kind, chunk, j)
                    if k == SLOTS - 1 and not (last and layer):
                        place_indices(0 if last else (s + 1) * SC, 0)
                    if layer == 0 and not last and k + REST_RING in FEATS_CUT:
                        cut_feats(s, k + REST_RING)
                    if not last:
                        for q in COUNTED.get(k - 1, ()):
                            m = (layer * STEPS + s) * PAIRS + q + PAIR_RING
                            make_pair(m, s + (q + PAIR_RING) // PAIRS, (q + PAIR_RING) % PAIRS)
                    if u is not None and k == PAIRS_ADDED:
                        add_pairs(layer, u)
                    if u is not None:
                        node_stage(layer, u, k, last)

            def node_trio(layer, u):
                node_inputs(layer, u)
                invert(layer, u)
                activate(layer, u)
                if layer == 0:
                    cut_h(u)
                else:
                    statistics(u)
                    normalize(u)

            def tried_round(layer, r):
                before = (layer * ROUNDS + r) * TRIED
                dve.wait_ge(window_summed, before + 1)
                dve.wait_ge(rel_ready, before + layer * ROUNDS + r + 1)
                nc.vector.tensor_copy(idx[:, 0, 0:GENERAL], src_idx[:, at(r * GENERAL, GENERAL)]).then_inc(idx_ready, 1)
                nc.vector.tensor_scalar(rel_w[:, :], dst_f[:, at(r * GENERAL, GENERAL)], float(P), None,
                                        ALU.add).then_inc(rel_ready, 1)
                with dve.Fori(0, TRIED) as w:
                    n = before + w
                    dve.wait_ge(window_summed, n + 1)
                    dve.wait_ge(rel_ready, n + layer * ROUNDS + r + 2)
                    for k in range(GENERAL):
                        last = nc.vector.tensor_scalar(onehot["gather"][:, k, :], column[:, 0:W], rel_w[:, k:k + 1],
                                                       None, ALU.is_equal)
                    last.then_inc(onehot_ready["gather"], 1)
                    dve.wait_ge(onehot_ready["gather"], n + 1)
                    nc.vector.tensor_scalar(rel_w[:, :], rel_w[:, :], float(W), None,
                                            ALU.subtract).then_inc(rel_ready, 1)
                    dve.wait_ge(window_summed, n + 2)
                    add_window(layer, "gather", w * W, ps_win[0]).then_inc(window_added, 1)

            dve.wait_ge(setup_done, 1)
            flag = load_flag(mybir.EngineType.DVE)
            with dve.If(flag == 0):
                place_indices(0, 0)
                for kind, chunk, j in LAST:
                    make_onehot(kind, chunk, j)
                for q in range(PAIR_RING):
                    make_pair(q, 0, q)
                for kind, chunk, j in ORDER:
                    if kind == "count":
                        make_onehot(kind, chunk, j)
                for layer in range(2):
                    step(layer, 0)
                    with dve.Fori(1, STEPS) as s:
                        step(layer, s, u=s - 1)
                    step(layer, STEPS, u=STEPS - 1, last=True)
                    activate(layer, TRIOS - 1, own=True)
                    if layer == 0:
                        cut_h(TRIOS - 1)
                    else:
                        statistics(TRIOS - 1)
                        normalize(TRIOS - 1)
                    if layer == 0:
                        dve.wait_ge(sums_cleared, TRIOS)
            with dve.Else():
                dve.sem_inc(window_summed, 1)
                dve.sem_inc(window_added, 1)
                dve.sem_inc(rel_ready, 1)
                for layer in range(2):
                    with dve.Fori(0, ROUNDS) as r:
                        tried_round(layer, r)
                    dve.wait_ge(window_added, (layer + 1) * ROUNDS * TRIED + 1)
                    node_trio(layer, 0)
                    with dve.Fori(1, TRIOS) as u:
                        node_trio(layer, u)
                    if layer == 0:
                        dve.wait_ge(sums_cleared, TRIOS)

        @block.scalar
        def _(act):
            for i in range(CUTS + 1):
                if i < CUTS:
                    t = slice(CUT * i, CUT * (i + 1))
                    act.wait_ge(x_staged[i], 16)
                    nc.scalar.copy(h_parts[:, t, 0, :], upper(x_stage[i])).then_inc(x_part[0], 1)
                if i:
                    t = slice(CUT * (i - 1), CUT * i)
                    act.wait_ge(x_rest, i)
                    nc.scalar.copy(h_parts[:, t, 1, :], upper(x_stage[i - 1])).then_inc(x_part[1], 1)

            def keep_counts(layer, s, q):
                g = layer * STEPS + s
                for b in range(BANKS):
                    act.wait_ge(piece_counted, (g * PAIRS + q) * BANKS + b + 1)
                    if q == 0 and b == 0 and not zero(g):
                        act.wait_ge(group_multiplied, g)
                    nc.scalar.copy(counts[:, q, b * PIECE:(b + 1) * PIECE],
                                   ps_count[:, b, 0:PIECE]).then_inc(piece_kept, 1)

            def take_degree(u, own=False):
                if not zero(u):
                    act.wait_ge(deg_turned, u)
                    act.wait_ge(turned_stored, 16 * (u - 1 if own else u))
                act.wait_ge(agg_summed, u + 1)
                act.sem_inc(act_step, 1)
                nc.scalar.copy(deg_row, sums[0:1, DEG, at(u * TRIO, TRIO)]).then_inc(deg_taken, 1)
                nc.scalar.copy(sums[:, ROW, at(u * TRIO, TRIO)], zeros[:, :]).then_inc(sums_cleared, 1)

            def scale(layer, u, own=False):
                n = layer * TRIOS + u
                act.wait_ge(node_out, n + 1)
                act.wait_ge(deg_inverted, n + 1)
                if not zero(n):
                    act.wait_ge(h_made, n)
                for t in range(3):
                    nc.scalar.activation(mean[:, t * D:(t + 1) * D], node_buffers(own)[3][:, 0, t * D:(t + 1) * D],
                                         ACT.Copy, scale=inv_now[:, int(own), t:t + 1]).then_inc(mean_made, 1)

            def keep_h(u):
                act.wait_ge(h_made, u + 1)
                if not zero(u):
                    act.wait_ge(parts_stored, 16 * u)
                nc.scalar.copy(row_parts[:, :, 0, :],
                               upper(h_row[:, :]).rearrange("p (t d) -> p t d", d=D)).then_inc(part_copied, 1)
                act.wait_ge(h_rest_made, u + 1)
                nc.scalar.copy(row_parts[:, :, 1, :],
                               upper(h_rest[:, :]).rearrange("p (t d) -> p t d", d=D)).then_inc(part_copied, 1)
                act.wait_ge(part_copied, 2 * (u + 1))
                act.wait_ge(last_part_made, u + 1)
                act.dma_start(by_tile(h_parts_rows[at(u * TRIO, TRIO), :]),
                              row_parts[:, :, :, :].rearrange("p t k d -> p t (k d)")).then_inc(parts_stored, 16)

            def keep_turned(u, own=False):
                act.wait_ge(h_turned, u + 1)
                if not zero(u):
                    act.wait_ge(turned_stored, 16 * u)
                nc.scalar.copy(turned[:, :], node_buffers(own)[3][:, 0, 0:TRIO]).then_inc(turned_kept, 1)
                act.wait_ge(turned_kept, u + 1)
                act.dma_start(h_cols[:, at(u * TRIO, TRIO)], turned[:, :]).then_inc(turned_stored, 16)

            def root(u):
                act.wait_ge(mv_made, 3 * (u + 1))
                nc.scalar.activation(std[:, :], mv[:, :, 1], ACT.Sqrt, bias=eps[:, :]).then_inc(std_made, 1)

            def store(u, first=0, full=3, tail=0):
                act.wait_ge(y_made, 3 * (u + 1))
                act.dma_start(by_tile(out[at(u * TRIO - P + first * P, (full - first) * P), :]),
                              res[:, first * D:full * D].rearrange("p (t d) -> p t d", d=D)).then_inc(out_stored, 16)
                if tail:
                    act.dma_start(out[N - tail:N, :], res[0:tail, full * D:(full + 1) * D]).then_inc(out_stored, 16)

            def store_any(u):
                if zero(u):
                    store(u, first=1)
                elif isinstance(u, int) and u == TRIOS - 1:
                    store(u, full=1, tail=N % P)
                else:
                    store(u)

            def step(layer, s, u=None):
                for q in range(PAIRS):
                    keep_counts(layer, s, q)
                    if q == DEGREES_TAKEN and u is not None and layer == 0:
                        take_degree(u)
                if u is not None:
                    scale(layer, u)
                    if layer == 0:
                        keep_h(u)
                        keep_turned(u)
                    else:
                        root(u)
                        store_any(u)

            def finish(layer, u, own=False):
                scale(layer, u, own)
                if layer == 0:
                    keep_h(u)
                    keep_turned(u, own)
                else:
                    root(u)
                    store_any(u)

            def node_trio(layer, u):
                if layer == 0:
                    take_degree(u)
                finish(layer, u)

            act.wait_ge(setup_done, 1)
            flag = load_flag(mybir.EngineType.Activation)
            with act.If(flag == 0):
                for layer in range(2):
                    step(layer, 0)
                    step(layer, 1, 0)
                    with act.Fori(2, STEPS) as s:
                        step(layer, s, s - 1)
                    if layer == 0:
                        take_degree(STEPS - 1)
                        take_degree(TRIOS - 1, own=True)
                    finish(layer, STEPS - 1)
                    finish(layer, TRIOS - 1, own=True)
            with act.Else():
                for layer in range(2):
                    node_trio(layer, 0)
                    with act.Fori(1, TRIOS - 1) as u:
                        node_trio(layer, u)
                    node_trio(layer, TRIOS - 1)
            act.wait_ge(out_stored, 16 * (TRIOS + 1))

        @block.tensor
        def _(pe):
            pe.wait_ge(setup_step, setup_marks["bases"])
            nc.tensor.matmul(ps_node[:, 0, 0:ALL_WINDOWS], ones[0:1, :], base_f[0:1, :],
                             start=True, stop=True).then_inc(bases_spread, 1)
            nc.tensor.matmul(ps_self[:, 0, 0:STEPS * PAIRS], ones[0:1, :],
                             pair_f[0:1, :, :].rearrange("o s q -> o (s q)"),
                             start=True, stop=True).then_inc(pairs_spread, 1)
            pe.wait_ge(setup_step, setup_marks["bad"])
            nc.tensor.matmul(ps_node[0:1, 0, 256:257], bad[:, :], ones[:, 0:1],
                             start=True, stop=True).then_inc(bad_counted, 1)

            def sum_window(layer, kind, ps, slot, feats_slot, n=SUB, rest=None):
                r0, f0 = SUB * slot, SUB * feats_slot
                parts = {
                    EDGE: lambda k: [feats[:, f0 + k, :]] if rest is None else [
                        upper(feats[:, f0 + k:f0 + k + 1, :])[:, 0, :], upper(feats_rest[:, SUB * rest + k, :]),
                        lower(feats[:, f0 + k:f0 + k + 1, :])[:, 0, :]],
                    ROW: lambda k: [rows[:, r0 + k, i * D:(i + 1) * D] for i in range(PARTS)],
                    DEG: lambda k: [upper(ones[:, :])],
                }
                for what, cut in parts.items():
                    if (layer and what != ROW) or (kind == "count" and what == ROW):
                        continue
                    lefts = [(left, k) for k in range(n) for left in cut(k)]
                    for i, (left, k) in enumerate(lefts):
                        right = onehot[kind][:, r0 + k, :]
                        last = nc.tensor.matmul(ps[:, 0, what * W:(what + 1) * W], left,
                                                right if what == EDGE and rest is None else upper(right),
                                                start=(i == 0), stop=(i == len(lefts) - 1))
                return last

            def count_pair(layer, s, q):
                n = (layer * STEPS + s) * PAIRS + q
                pe.wait_ge(codes_ready, n + 1)
                for b in range(BANKS):
                    if not zero(n):
                        pe.wait_ge(piece_kept, (n - 1) * BANKS + b + 1)
                    for c in range(2):
                        last = nc.tensor.matmul(ps_count[:, b, 0:PIECE], is_lane[:, q % PAIR_RING, c, :],
                                                is_code[:, q % PAIR_RING, c, b * PIECE:(b + 1) * PIECE],
                                                start=(c == 0), stop=(c == 1))
                    last.then_inc(piece_counted, 1)

            def multiply(layer, s, i):
                g = layer * STEPS + s
                if i == 0:
                    pe.wait_ge(piece_kept, (g + 1) * PAIRS * BANKS)
                    if not zero(g):
                        pe.wait_ge(pair_added, g * PAIRS)
                    if layer:
                        pe.wait_ge(parts_loaded, 16 * CUTS)
                for t in range(CUT * i, CUT * (i + 1)):
                    for k in range(PARTS):
                        last = nc.tensor.matmul(ps_dense[:, 0, 0:PAIRS * WP], h_parts[:, t, k, :],
                                                counts[:, :, t * WP:(t + 1) * WP],
                                                start=(t == 0 and k == 0), stop=(t == SRC_TILES - 1 and k == PARTS - 1))
                if i == CUTS - 1:
                    last.then_inc(group_multiplied, 1)

            def turn_degrees(u, own=False):
                if not (own or zero(u)):
                    pe.wait_ge(h_made, u)
                pe.wait_ge(deg_taken, u + 1)
                for t in range(3):
                    last = nc.tensor.matmul(node_buffers(own)[4][:, 0, TRIO + t:TRIO + t + 1],
                                            deg_row[:, t * P:(t + 1) * P], ones[0:1, 0:1], start=True, stop=True)
                last.then_inc(deg_turned, 1)

            def node_products(layer, u, own=False):
                n = layer * TRIOS + u
                msg, con, iso, of_messages, of_self = node_buffers(own)
                if zero(u):
                    pe.wait_ge(wts_loaded, 16 * 3 * (layer + 1))
                if not (own or zero(n)):
                    pe.wait_ge(h_made, n)
                    pe.wait_ge(turned_kept, u if layer == 0 else TRIOS)
                if layer == 0:
                    pe.wait_ge(deg_clamped, u + 1)
                pe.wait_ge(node_in, n + 1)
                for t in range(3):
                    for k, left in ((0, msg), (1, con), (2, iso)):
                        last = nc.tensor.matmul((of_self if k else of_messages)[:, 0, t * D:(t + 1) * D],
                                                left[:, t * P:(t + 1) * P], wts[:, k, :],
                                                start=(k != 2), stop=(k != 1))
                last.then_inc(node_out, 1)

            def turn(u, own=False):
                pe.wait_ge(h_made, u + 1)
                if not (own or zero(u)):
                    pe.wait_ge(turned_kept, u)
                for t in range(3):
                    last = nc.tensor.transpose(node_buffers(own)[3][:, 0, t * P:(t + 1) * P],
                                               h_row[:, t * D:(t + 1) * D], ident[:, :])
                last.then_inc(h_turned, 1)

            def node_stage(layer, u, k, last):
                when = (LAST_WHEN if last else WHEN)[layer]
                if when.get("degrees") == k:
                    turn_degrees(u)
                if when["products"] == k:
                    node_products(layer, u)
                if last and k == SLOTS - 1:
                    pe.wait_ge(window_added, windows_before(layer, STEPS) + SLOTS)
                    if layer == 0:
                        turn_degrees(TRIOS - 1, own=True)
                    node_products(layer, TRIOS - 1, own=True)
                if when.get("turn") == k:
                    turn(u)

            def step(layer, s, u=None, last=False):
                before = windows_before(layer, s)
                pieces = list(range(CUTS))
                for k, (kind, chunk, j) in enumerate(order(layer, None if last else s)):
                    n = before + k
                    nth = 2 * SLOTS * s + j + (0 if chunk < GC else SLOTS)
                    if kind == "gather":
                        pe.wait_ge(onehot_ready[kind], layer * GATHERED + nth + 1)
                        uses = layer * GATHERED // SLOTS + 2 * s + (0 if chunk < GC else 1)
                        pe.wait_ge(rows_gathered[j], 16 * SUB * (uses + 1))
                    else:
                        pe.wait_ge(onehot_ready[kind], s * SLOTS + j + 1)
                    if layer == 0:
                        pe.wait_ge(feats_loaded[k % RING], 16 * (s * (SW // RING) + k // RING + 1))
                    if not (isinstance(n, int) and n < 2):
                        pe.wait_ge(window_added, n - 1)
                    rest = None
                    if layer == 0 and k in FEATS_CUT and not last:
                        i = FEATS_CUT.index(k)
                        pe.wait_ge(feats_cut, s * len(FEATS_CUT) + i + 1)
                        rest = i % REST_RING
                    sum_window(layer, kind, ps_win[k % 2], j, k % RING, rest=rest).then_inc(window_summed, 1)
                    if not last:
                        for q in COUNTED.get(k, ()):
                            count_pair(layer, s, q)
                        if k > LAST_COUNTED:
                            for i in [pieces.pop(0) for _ in range(min(len(pieces), 1 if layer == 0 else 2))]:
                                multiply(layer, s, i)
                    if u is not None:
                        node_stage(layer, u, k, last)

            def tried_round(layer, r):
                for j in range(2):
                    if layer == 0:
                        pe.wait_ge(feats_loaded[j], 16 * (r + 1))
                    pe.wait_ge(rows_gathered[j], 16 * SUB * (layer * ROUNDS + r + 1))
                pe.sem_inc(pe_step, 1)
                with pe.Fori(0, TRIED) as w:
                    n = (layer * ROUNDS + r) * TRIED + w
                    pe.wait_ge(onehot_ready["gather"], n + 1)
                    pe.wait_ge(window_added, n + 1)
                    sum_window(layer, "gather", ps_win[0], 0, 0, n=GENERAL).then_inc(window_summed, 1)

            pe.wait_ge(setup_done, 1)
            flag = load_flag(mybir.EngineType.PE)
            with pe.If(flag == 0):
                for layer in range(2):
                    step(layer, 0)
                    with pe.Fori(1, STEPS) as s:
                        step(layer, s, u=s - 1)
                    step(layer, STEPS, u=STEPS - 1, last=True)
                    if layer == 0:
                        turn(TRIOS - 1, own=True)
                        pe.wait_ge(turned_kept, TRIOS)
            with pe.Else():
                for layer in range(2):
                    with pe.Fori(0, ROUNDS) as r:
                        tried_round(layer, r)
                    if layer == 0:
                        turn_degrees(0)
                    node_products(layer, 0)
                    if layer == 0:
                        turn(0)
                    with pe.Fori(1, TRIOS) as u:
                        if layer == 0:
                            turn_degrees(u)
                        node_products(layer, u)
                        if layer == 0:
                            turn(u)


_ORDER = ["x_rows", "x_cols", "src", "dst", "edges", "wn0", "ws0", "wi0", "wn1", "ws1", "wi1"]


def kernel(**inputs):
    import numpy as _np
    import concourse.bacc as _bacc
    from concourse import mybir as _mybir
    from concourse.bass_utils import run_bass_kernel_spmd as _run

    x = _np.asarray(inputs["x"])
    src, dst = _np.asarray(inputs["src"]), _np.asarray(inputs["dst"])
    feats = _np.asarray(inputs["edge_attr_128"])
    P, GROUP = 128, 2048
    n, e = x.shape[0], src.shape[0]
    before, after, e_pad = P, -(n + P) % (3 * P), -e % GROUP
    x_rows = _np.pad(x, ((before, after), (0, 0)))
    lay = {
        "x_rows": x_rows,
        "x_cols": x_rows.T,
        "src": _np.pad(src, (0, e_pad)).reshape(-1, P).T,
        "dst": _np.pad(dst, (0, e_pad), constant_values=1 << 20).reshape(-1, P).T,
        "edges": _np.pad(feats, ((0, e_pad), (0, 0))).reshape(-1, P, feats.shape[1]).transpose(1, 0, 2),
    }
    for layer in range(2):
        for kind in "nsi":
            lay[f"w{kind}{layer}"] = _np.asarray(inputs[f"L0_gnn_W{kind}{layer}"]).T

    nc = _bacc.Bacc("TRN2", target_bir_lowering=False, num_devices=1)
    arrays, args = {}, []
    for name in _ORDER:
        a = _np.ascontiguousarray(lay[name])
        arrays[f"in_{name}_dram"] = a
        args.append(nc.dram_tensor(f"in_{name}_dram", a.shape, _mybir.dt.from_np(a.dtype), kind="ExternalInput").ap())
    args.append(nc.dram_tensor("out_0_dram", x.shape, _mybir.dt.float32, kind="ExternalOutput").ap())
    gnn_resnorm_kernel(nc, *args)
    r = _run(nc, [arrays], core_ids=[0])
    return r.results[0]["out_0_dram"]
```
